# Optimizing a Trainium2 kernel written in Bass

```python
import numpy as np
import jax
import jax.numpy as jnp

def _softmax(x, axis=-1):
    return jax.nn.softmax(x, axis=axis)

def _gelu(x):
    return jax.nn.gelu(x, approximate=True)

def _silu(x):
    return jax.nn.silu(x)

def _sigmoid(x):
    return jax.nn.sigmoid(x)

def _layernorm(x, axis=-1, eps=1e-05):
    m = jnp.mean(x, axis=axis, keepdims=True)
    v = jnp.var(x, axis=axis, keepdims=True)
    return (x - m) / jnp.sqrt(v + eps)

def _scatter_add(tgt, idx, src, axis=0):
    return tgt.at[idx].add(src)

def _segment_sum(src, seg, n):
    return jax.ops.segment_sum(src, seg, n)
kernel_name = 'mk_adaln_d1_jaxref_r4_17a8f1'

def setup_inputs(seed: int=0):
    np.random.seed(seed)
    _w = jnp.asarray

    def _L0_attn_setup():
        import jax, jax.numpy as jnp
        import numpy as np
        B, S, D_MODEL, D_K = (4, 512, 256, 1)
        D_QKV = D_MODEL * D_K
        MASK_NEG = -9000000000000000.0

        def _scaled_dot_product_attention(q, k, v):
            d_k = k.shape[-1]
            scores = jnp.einsum('bqd,bkd->bqk', q, k) / jnp.sqrt(jnp.float32(d_k))
            scores = jnp.triu(scores, k=0)
            scores = jnp.where(scores == 0, MASK_NEG, scores)
            attn = jax.nn.softmax(scores, axis=-1)
            return jnp.einsum('bqk,bkd->bqd', attn, v)
        key = jax.random.key(seed)
        kx, kw = jax.random.split(key)
        x = jax.random.normal(kx, (B, S, D_MODEL), dtype=jnp.float32)
        W = jax.random.normal(kw, (D_MODEL, 3 * D_QKV), dtype=jnp.float32) * (1.0 / np.sqrt(D_MODEL))
        return {'x': x, 'W': W}
    _L0_attn_in = _L0_attn_setup()

    def _L0_ffn_setup():
        import jax, jax.numpy as jnp
        import numpy as np
        TOP_K = 2
        key = jax.random.key(seed)
        k1, k2, k3, k4, k5 = jax.random.split(key, 5)
        B, S, D, F, E = (2, 256, 256, 512, 8)
        return {'x': jax.random.normal(k1, (B, S, D), dtype=jnp.float32), 'router_kernel_DE': jax.random.normal(k2, (D, E), dtype=jnp.float32) * 0.02, 'kernel_gating_EDF': jax.random.normal(k3, (E, D, F), dtype=jnp.float32) * 0.02, 'kernel_up_EDF': jax.random.normal(k4, (E, D, F), dtype=jnp.float32) * 0.02, 'kernel_down_EFD': jax.random.normal(k5, (E, F, D), dtype=jnp.float32) * 0.02}
    _L0_ffn_in = _L0_ffn_setup()
    _L0_c = _w((lambda *s: np.random.randn(*s).astype(np.float32) * 0.05)(4, 256))
    _L0_wmod = _w((lambda *s: np.random.randn(*s).astype(np.float32) * 0.05)(256, 6 * 256) * 256 ** (-0.5))
    _d = {'L0_attn_x': _L0_attn_in['x'], 'L0_attn_W': _L0_attn_in['W'], 'L0_ffn_router_kernel_DE': _L0_ffn_in['router_kernel_DE'], 'L0_ffn_kernel_gating_EDF': _L0_ffn_in['kernel_gating_EDF'], 'L0_ffn_kernel_up_EDF': _L0_ffn_in['kernel_up_EDF'], 'L0_ffn_kernel_down_EFD': _L0_ffn_in['kernel_down_EFD'], 'L0_c': _L0_c, 'L0_wmod': _L0_wmod}
    _x0 = _d['L0_attn_x']
    _d['L0_attn_x'] = jax.random.normal(jax.random.fold_in(jax.random.key(seed), 1), (4, 1024, 256), dtype=_x0.dtype)
    del _x0
    return _d

def reference(L0_attn_x, L0_attn_W, L0_ffn_router_kernel_DE, L0_ffn_kernel_gating_EDF, L0_ffn_kernel_up_EDF, L0_ffn_kernel_down_EFD, L0_c, L0_wmod):

    def _L0_attn_ref(x, W):
        import jax, jax.numpy as jnp
        import numpy as np
        B, S, D_MODEL, D_K = (4, 512, 256, 1)
        D_QKV = D_MODEL * D_K
        MASK_NEG = -9000000000000000.0

        def _scaled_dot_product_attention(q, k, v):
            d_k = k.shape[-1]
            scores = jnp.einsum('bqd,bkd->bqk', q, k) / jnp.sqrt(jnp.float32(d_k))
            scores = jnp.triu(scores, k=0)
            scores = jnp.where(scores == 0, MASK_NEG, scores)
            attn = jax.nn.softmax(scores, axis=-1)
            return jnp.einsum('bqk,bkd->bqd', attn, v)
        qkv = jnp.einsum('bsd,df->bsf', x, W)
        q, k, v = jnp.split(qkv, 3, axis=-1)
        return _scaled_dot_product_attention(q, k, v)

    def _L0_ffn_ref(x, router_kernel_DE, kernel_gating_EDF, kernel_up_EDF, kernel_down_EFD):
        import jax, jax.numpy as jnp
        import numpy as np
        TOP_K = 2
        E = router_kernel_DE.shape[-1]
        x = x.astype(jnp.float32)
        logits_BSE = jnp.einsum('BSD,DE->BSE', x, router_kernel_DE)
        probs_BSE = jax.nn.softmax(logits_BSE.astype(jnp.float32), axis=-1)
        weights_BSK, indices_BSK = jax.lax.top_k(probs_BSE, TOP_K)
        norm_weights_BSK = jax.nn.softmax(weights_BSK, axis=-1)
        one_hot_BSKE = jax.nn.one_hot(indices_BSK, num_classes=E, dtype=x.dtype)
        full_weights_BSE = jnp.sum(one_hot_BSKE * norm_weights_BSK[..., None], axis=2)
        gating_BSEF = jnp.einsum('BSD,EDF->BSEF', x, kernel_gating_EDF)
        act_BSEF = jax.nn.silu(gating_BSEF)
        up_BSEF = jnp.einsum('BSD,EDF->BSEF', x, kernel_up_EDF)
        fuse_BSEF = act_BSEF * up_BSEF
        down_BSED = jnp.einsum('BSEF,EFD->BSED', fuse_BSEF, kernel_down_EFD)
        out_BSD = jnp.einsum('BSED,BSE->BSD', down_BSED, full_weights_BSE)
        return out_BSD.astype(jnp.float32)
    x = L0_attn_x
    mod = (_silu(L0_c) @ L0_wmod).reshape(L0_c.shape[0], 6, 1, -1)
    sa, ca, ga, sb, cb, gb = (mod[:, 0], mod[:, 1], mod[:, 2], mod[:, 3], mod[:, 4], mod[:, 5])
    ga = (2 * (ga >= 0) - 1) * jnp.maximum(jnp.abs(ga), 0.25)
    gb = (2 * (gb >= 0) - 1) * jnp.maximum(jnp.abs(gb), 0.25)
    h = _layernorm(x, axis=-1) * (1 + ca) + sa
    x = x + ga * _L0_attn_ref(h, L0_attn_W)
    h = _layernorm(x, axis=-1) * (1 + cb) + sb
    x = x + gb * _L0_ffn_ref(h, L0_ffn_router_kernel_DE, L0_ffn_kernel_gating_EDF, L0_ffn_kernel_up_EDF, L0_ffn_kernel_down_EFD)
    return x

_drawn_inputs = setup_inputs


def setup_inputs(seed=0):
    import zlib

    import numpy as np

    out = dict(_drawn_inputs(seed))
    spreads = {}
    factors = {'L0_ffn_router_kernel_DE': 8.0,
     'L0_ffn_kernel_gating_EDF': 8.0,
     'L0_ffn_kernel_up_EDF': 8.0,
     'L0_ffn_kernel_down_EFD': 8.0}
    for name, (base, spread) in spreads.items():
        noise = np.random.default_rng([zlib.crc32(name.encode()), seed]).standard_normal(out[name].shape)
        drawn = base * np.exp(spread * noise) if base else spread * noise
        out[name] = jnp.asarray(drawn.astype(out[name].dtype))
    for name, factor in factors.items():
        out[name] = (out[name] * factor).astype(out[name].dtype)
    return out
```

```python
from contextlib import ExitStack

import concourse.bass as bass
from concourse import mybir

fp32 = mybir.dt.float32
bf16 = mybir.dt.bfloat16
i32 = mybir.dt.int32
ALU = mybir.AluOpType
ACT = mybir.ActivationFunctionType
AX = mybir.AxisListType

P = 128
B, S, D = 4, 1024, 256
E, F = 8, 512
DC, FC = D // P, F // P
NT = S // P
TOK = B * S
NTT = TOK // P
MASK_NEG = -9000000000000000.0
EPS = 1e-5
REG = TOK + P
DUMMY = E * REG
TILES = 2 * TOK // P + E - 1

ORDER = [7, 0, 6, 1, 5, 2, 4, 3]
assert sorted(ORDER) == list(range(NT))
GROUP = 4


def groups_of(pos):
    n = NT - ORDER[pos]
    return [(g, min(GROUP, n - g)) for g in range(0, n, GROUP)]


def transpose_uses():
    uses = [("x", t) for t in range(NT)]
    for k in range(-1, NT + 3):
        if 0 <= k < NT:
            uses += [("p", k, g) for g, _ in groups_of(k)]
        if 0 <= k - 3 < NT:
            uses.append(("h", k - 3))
    return uses


TP_USES = transpose_uses()
TP_AT = {use: n for n, use in enumerate(TP_USES)}
TP_HALF = len(TP_USES) // 2
assert len(TP_USES) % 2 == 0


def misc_uses():
    uses = ["vsum"]
    for k in range(-1, NT + 4):
        if 0 <= k < NT and ORDER[k] > 0:
            uses.append(("pm", k))
        if 0 <= k - 4 < NT:
            uses.append(("lg", k - 4))
    return uses + ["rank"]


MISC_USES = misc_uses()
MISC_AT = {use: n for n, use in enumerate(MISC_USES)}
SC_HALF = (4 + NT) // 2
STEPS = range(-1, NT + 4)


def nth(batch, per_batch, k):
    return batch * per_batch + (k + 1)


def build(nc, x, attn_w, router, w_gate, w_up, w_down, cond, w_mod, out):
    ctx = ExitStack()
    with ctx:
        def sb(name, shape, dt=fp32):
            return ctx.enter_context(nc.sbuf_tensor(name, shape, dt))

        def pb(name, shape):
            return ctx.enter_context(nc.psum_tensor(name, shape, fp32))

        def sem(name):
            return ctx.enter_context(nc.semaphore(name))

        rows_hbm = nc.dram_tensor("rows_hbm", [E * REG + P, D], fp32, kind="Internal").ap()
        y_hbm = nc.dram_tensor("y_hbm", [TILES * P, D], fp32, kind="Internal").ap()
        x1_hbm = nc.dram_tensor("x1_hbm", [TOK, D], fp32, kind="Internal").ap()

        gate_sb = sb("gate_sb", [P, E, DC, F])
        up_sb = sb("up_sb", [P, E, DC, F])
        down_sb = sb("down_sb", [P, E, FC, D])

        ident = sb("ident", [P, P])
        upper = sb("upper", [P, P])
        before = sb("before", [P, P], bf16)
        ones = sb("ones", [P, P], bf16)
        neg_col = sb("neg_col", [P, 1])
        zeros_row = sb("zeros_row", [P, D])
        minus_half = sb("minus_half", [P, NT])
        region = sb("region", [P, E])
        choice_rank = sb("choice_rank", [P, E])
        int_tmp = sb("int_tmp", [P, E * 32], i32)

        attn_sb = sb("attn_sb", [P, DC, 3 * D])
        qk_sb = sb("qk_sb", [P, DC, D])
        router_sb = sb("router_sb", [P, DC, E])
        mod_rows = sb("mod_rows", [P, B, 4, D])
        mod_cols = sb("mod_cols", [P, 2 * DC, B])
        mod_now = sb("mod_now", [P, 2 * DC])
        silu_c = sb("silu_c", [P, DC, B])
        xb = sb("xb", [P, NT, D])
        hT = sb("hT", [P, DC, S])
        qv = sb("qv", [P, DC * S + NT * D])
        qT = qv[:, 0:DC * S].rearrange("p (c s) -> p c s", c=DC)
        v_sb = qv[:, DC * S:].rearrange("p (t d) -> p t d", t=NT)
        pen = sb("pen", [P, S])
        prob = sb("prob", [P, 2, S])
        probT = sb("probT", [P, 2, S])
        xr = sb("xr", [P, 4, D])
        x1 = sb("x1", [P, 2, D])
        h2 = sb("h2", [P, NT, D])
        h2T = sb("h2T", [P, 2, D])
        hsum = sb("hsum", [P, DC, NT])
        vsum = sb("vsum", [NT, D])
        stats = sb("stats", [P, NT, 6])
        mv = sb("mv", [P, NT, 2])
        veps = sb("veps", [P, NT])
        rstd = sb("rstd", [P, NT])
        newt = sb("newt", [P, NT])
        stats2 = sb("stats2", [P, 6])
        mv2 = sb("mv2", [P, 2, 2])
        small2 = sb("small2", [P, 4])
        negmax = sb("negmax", [P, NT])
        rowsum = sb("rowsum", [P, NT])
        rinv = sb("rinv", [P, NT])
        pm = sb("pm", [P, NT])
        pm_rows = sb("pm_rows", [P, NT, NT])
        pmT = sb("pmT", [NT, 2, P])

        lg = sb("lg", [P, NT, E])
        rt = [sb(f"rt{n}", [P, NT, E]) for n in range(3)]
        rs = [sb(f"rs{n}", [P, NT]) for n in range(4)]
        pick = sb("pick", [P, 2, NTT, E])
        slot = sb("slot", [P, 2, NTT])
        weight = sb("weight", [P, 2, NTT])
        slot_i = sb("slot_i", [P, 2, NTT], i32)
        slot_now = sb("slot_now", [P, 2, NT], i32)
        chosen = sb("chosen", [P, NT, E], bf16)
        seen = sb("seen", [P, NT + 1, E], bf16)

        count = sb("count", [P, E])
        tiles_of = sb("tiles_of", [P, E])
        end_of = sb("end_of", [P, E])
        start_delta = sb("start_delta", [P, E])
        steps32 = sb("steps32", [P, NTT])
        lower8 = sb("lower8", [P, E, E])
        tile_no = sb("tile_no", [1, TILES])
        tile_exp = sb("tile_exp", [1, TILES])
        tile_row = sb("tile_row", [1, TILES])
        tile_exp_i = sb("tile_exp_i", [1, TILES], i32)
        tile_row_i = sb("tile_row_i", [1, TILES], i32)
        pad_i = sb("pad_i", [1, E], i32)

        hin = xb[:, 0:2, :]
        hinT = hT[:, 0, 0:2 * D].rearrange("p (r d) -> p r d", r=2)
        act_sb = prob[:, 0, :].rearrange("p (r f) -> p r f", r=2)
        fused = prob[:, 1, :].rearrange("p (r f) -> p r f", r=2)
        fusedT = probT[:, 0, :].rearrange("p (r f) -> p r f", r=2)
        y_sb = h2[:, 0:2, :]
        grid = qv[:, 0:E * TILES]
        grid2 = pen[:, 0:E * TILES]
        ya = qT.rearrange("p c s -> p (c s)").rearrange("p (r d) -> p r d", d=D)
        yb = v_sb
        xc = xb
        oc = h2

        tp = [pb(f"tp{n}", [P, 512]) for n in range(2)]
        sc = [pb(f"sc{n}", [P, 1024]) for n in range(2)]
        po = pb("po", [P, 512])
        pmisc = pb("pmisc", [P, 512])

        attn_in, router_in, cond_in, wmod_in = sem("attn_in"), sem("router_in"), sem("cond_in"), sem("wmod_in")
        expert_in, zeros_out = sem("expert_in"), sem("zeros_out")
        consts_made, pool_done, dve_done = sem("consts_made"), sem("pool_done"), sem("dve_done")
        pool_passed = sem("pool_passed")
        setup_pe, setup_dve, setup_act = sem("setup_pe"), sem("setup_dve"), sem("setup_act")
        x_in, xr_in = sem("x_in"), [sem(f"xr_in{n}") for n in range(4)]
        stats_made, xn_made = sem("stats_made"), sem("xn_made")
        mod_now_made = sem("mod_now_made")
        tp_full, tp_free = [sem(f"tp_full{n}") for n in range(2)], [sem(f"tp_free{n}") for n in range(2)]
        sc_full, sc_free = [sem(f"sc_full{n}") for n in range(2)], [sem(f"sc_free{n}") for n in range(2)]
        po_full, po_free = sem("po_full"), sem("po_free")
        misc_full, misc_free = sem("misc_full"), sem("misc_free")
        hsum_made = sem("hsum_made")
        masked, exp_made, pm_made = sem("masked"), sem("exp_made"), sem("pm_made")
        x1_made, x1_stored = sem("x1_made"), [sem(f"x1_stored{n}") for n in range(2)]
        mv2_made, h2_made = sem("mv2_made"), sem("h2_made")
        routed_exp, exp_routed = sem("routed_exp"), sem("exp_routed")
        chosen_made, slots_made, scattered = sem("chosen_made"), sem("slots_made"), sem("scattered")
        indices_used = sem("indices_used")
        table_made, padded = sem("table_made"), sem("padded")
        hin_in = [sem(f"hin_in{n}") for n in range(2)]
        hTp_full = sem("hTp_full")
        hinT_made = sem("hinT_made")
        gu_full, act_made, fused_made = sem("gu_full"), sem("act_made"), sem("fused_made")
        fTp_full, fusedT_made, y_full, y_made = sem("fTp_full"), sem("fusedT_made"), sem("y_full"), sem("y_made")
        y_out = [sem(f"y_out{n}") for n in range(2)]
        ya_in, yb_in = [sem(f"ya_in{n}") for n in range(8)], [sem(f"yb_in{n}") for n in range(8)]
        xc_in, o_made = [sem(f"xc_in{n}") for n in range(8)], sem("o_made")
        out_done = [sem(f"out_done{n}") for n in range(8)]
        y_slots_made = sem("y_slots_made")

        block = ctx.enter_context(nc.Block())

        @block.sync
        def _(sp):
            sp.dma_start(attn_sb[:, :, :], attn_w.rearrange("(c p) n -> p c n", p=P)).then_inc(attn_in, 16)
            wmod_sb = qv[:, 0:DC * 6 * D].rearrange("p (c n) -> p c n", c=DC)
            sp.dma_start(prob[0:B, 0, 0:D], cond[:, :]).then_inc(cond_in, 16)
            sp.dma_start(wmod_sb, w_mod.rearrange("(c p) n -> p c n", p=P)).then_inc(wmod_in, 16)
            sp.dma_start(xb[:, :, :], x[0, :, :].rearrange("(t p) d -> p t d", p=P)).then_inc(x_in, 16)
            sp.dma_start(router_sb[:, :, :], router.rearrange("(c p) n -> p c n", p=P)).then_inc(router_in, 16)
            for e in range(E):
                sp.dma_start(gate_sb[:, e, :, :], w_gate[e].rearrange("(c p) n -> p c n", p=P)).then_inc(expert_in, 16)
                sp.dma_start(up_sb[:, e, :, :], w_up[e].rearrange("(c p) n -> p c n", p=P)).then_inc(expert_in, 16)
                sp.dma_start(down_sb[:, e, :, :], w_down[e].rearrange("(c p) n -> p c n", p=P)).then_inc(expert_in, 16)
            sp.wait_ge(consts_made, 1)
            sp.dma_start(rows_hbm[DUMMY:DUMMY + P, :], zeros_row[:, :]).then_inc(zeros_out, 16)

            def batch(b, last):
                if not last:
                    for n in range(2):
                        sp.wait_ge(tp_full[n], nth(b, TP_HALF, NT // 2 - 1))
                    sp.dma_start(xb[:, :, :], x[bass.ds(b + 1, 1), :, :].rearrange("a (t p) d -> p (a t) d", p=P)
                                 ).then_inc(x_in, 16)
                for k in STEPS:
                    if 0 <= k + 1 < NT:
                        pos = k + 1
                        sp.wait_ge(x1_made, nth(b, NT, pos))
                        tile = b * NT + ORDER[pos]
                        sp.dma_start(xr[:, pos % 4, :], x_rows(tile)).then_inc(xr_in[pos % 4], 16)
                    if 0 <= k - 1 < NT:
                        pos = k - 1
                        sp.wait_ge(x1_made, nth(b, NT, pos + 4))
                        tile = b * NT + ORDER[pos]
                        sp.dma_start(x1_hbm[bass.ds(tile * P, P), :], x1[:, pos % 2, :]).then_inc(x1_stored[pos % 2], 16)

            def x_rows(tile):
                return x.rearrange("b s d -> (b s) d")[bass.ds(tile * P, P), :]

            with sp.Fori(0, B - 1) as b:
                batch(b, False)
            batch(B - 1, True)

            sp.wait_ge(table_made, 2)
            for e in range(E):
                first = sp.value_load(pad_i[0:1, e:e + 1], min_val=0, max_val=E * REG)
                sp.dma_start(rows_hbm[bass.ds(first, P), :], zeros_row[:, :]).then_inc(padded, 16)
            sp.wait_ge(padded, 16 * E)
            sp.wait_ge(scattered, 16 * 2 * NTT)
            sp.wait_ge(zeros_out, 16)

            def load_rows(t, slot_no):
                first = sp.value_load(tile_row_i[0:1, bass.ds(t, 1)], min_val=0, max_val=DUMMY)
                sp.dma_start(hin[:, slot_no, :], rows_hbm[bass.ds(first, P), :]).then_inc(hin_in[slot_no], 16)

            def store_y(t, slot_no):
                sp.wait_ge(y_made, t + 1)
                sp.dma_start(y_hbm[bass.ds(t * P, P), :], y_sb[:, slot_no, :]).then_inc(y_out[slot_no], 16)

            load_rows(0, 0)
            load_rows(1, 1)

            def step(t, par):
                sp.wait_ge(hTp_full, t + 1)
                load_rows(t + 2, par)

            step(0, 0)
            with sp.Fori(0, (TILES - 3) // 2) as i:
                for u in range(2):
                    step(2 * i + 1 + u, (1 + u) % 2)
                    store_y(2 * i + u, u % 2)
            for t in range(TILES - 3, TILES):
                store_y(t, t % 2)
            for n in range(2):
                sp.wait_ge(y_out[n], 16 * ((TILES + 1 - n) // 2) + 16)
                sp.wait_ge(x1_stored[n], 16 * (NTT // 2) + 16)
            for t in range(NTT + 6):
                if t < NTT:
                    n = t % 8
                    if t >= 8:
                        sp.wait_ge(o_made, t - 7)
                    sp.dma_start(xc[:, n, :], x1_hbm[t * P:(t + 1) * P, :]).then_inc(xc_in[n], 16)
                if t >= 6:
                    u = t - 6
                    sp.wait_ge(o_made, u + 1)
                    sp.dma_start(out.rearrange("b s d -> (b s) d")[u * P:(u + 1) * P, :], oc[:, u % 8, :]
                                 ).then_inc(out_done[u % 8], 16)
            for n in range(8):
                sp.wait_ge(out_done[n], 16 * (NTT // 8))

        @block.gpsimd
        def _(pool):
            done = [0]

            def link(ins):
                done[0] += 1
                ins.then_inc(pool_done, 1)
                pool.wait_ge(pool_done, done[0])

            def passed():
                pool.sem_inc(pool_passed, 1)

            pool.memset(zeros_row[:, :], 0.0).then_inc(consts_made, 1)
            link(pool.memset(ident[:, :], 0.0))
            link(pool.affine_select(out=ident[:, :], in_=ident[:, :], compare_op=ALU.not_equal, fill=1.0, base=0,
                                    pattern=[[-1, P]], channel_multiplier=1))
            link(pool.memset(upper[:, :], 1.0))
            link(pool.affine_select(out=upper[:, :], in_=upper[:, :], compare_op=ALU.is_ge, fill=0.0, base=0,
                                    pattern=[[1, P]], channel_multiplier=-1))
            link(pool.memset(before[:, :], 1.0))
            link(pool.affine_select(out=before[:, :], in_=before[:, :], compare_op=ALU.is_ge, fill=0.0, base=-1,
                                    pattern=[[1, P]], channel_multiplier=-1))
            link(pool.memset(ones[:, :], 1.0))
            link(pool.memset(neg_col[:, :], MASK_NEG))
            link(pool.memset(minus_half[:, :], -0.5))
            link(pool.memset(pm_rows[:, :, :].rearrange("p a b -> p (a b)"), 0.0))
            link(pool.memset(seen[:, 0, :], 0.0))
            link(pool.memset(lower8[:, :, :].rearrange("p a b -> p (a b)"), 1.0))
            link(pool.affine_select(out=lower8[:, :, :], in_=lower8[:, :, :], compare_op=ALU.is_ge, fill=0.0, base=0,
                                    pattern=[[1, E], [-1, E]], channel_multiplier=0))
            for dst, step_of, n, base in ((region, REG, E, 0), (choice_rank, -1, E, E), (steps32, P, NTT, 0)):
                link(pool.iota(int_tmp[:, 0:n], pattern=[[step_of, n]], base=base, channel_multiplier=0))
                link(pool.tensor_copy(dst[:, :], int_tmp[:, 0:n]))
            link(pool.iota(int_tmp[0:1, 0:TILES], pattern=[[1, TILES]], base=0, channel_multiplier=0))
            link(pool.tensor_copy(tile_no[:, :], int_tmp[0:1, 0:TILES]))
            pool.nop().then_inc(consts_made, 1)
            assert done[0] == 21, done[0]

            def rsqrt(var, n, v, r, t, count_of):
                count_of(pool.tensor_scalar(v, var, EPS, None, ALU.add))
                count_of(pool.tensor_tensor(r, v, minus_half[:, 0:n], ALU.pow))
                count_of(pool.tensor_tensor(t, r, r, ALU.mult))
                count_of(pool.tensor_tensor(t, t, v, ALU.mult))
                count_of(pool.tensor_scalar(t, t, -0.5, 1.5, ALU.mult, ALU.add))
                count_of(pool.tensor_tensor(r, r, t, ALU.mult))

            def normalise(b, count_of):
                pool.wait_ge(stats_made, nth(b, 1, 0))
                passed()
                rsqrt(mv[:, :, 1], NT, veps[:, :], rstd[:, :], newt[:, :], count_of)
                for t in range(NT):
                    pool.tensor_scalar(xb[:, t, :], xb[:, t, :], mv[:, t, 0:1], rstd[:, t:t + 1],
                                       ALU.subtract, ALU.mult).then_inc(xn_made, 1)

            normalise(0, link)

            def batch(b, last):
                at = [0]
                pool.sem_clear(pool_done)

                def link(ins):
                    at[0] += 1
                    ins.then_inc(pool_done, 1)
                    pool.wait_ge(pool_done, at[0])

                for k in STEPS:
                    if 0 <= k - 1 < NT:
                        pos = k - 1
                        qi = ORDER[pos]
                        m = mv2[:, pos % 2, :]
                        pool.wait_ge(mv2_made, nth(b, NT, pos))
                        passed()
                        rsqrt(m[:, 1:2], 1, small2[:, 0:1], small2[:, 1:2], small2[:, 2:3], link)
                        link(pool.tensor_scalar(h2[:, qi, :], x1[:, pos % 2, :], m[:, 0:1], small2[:, 1:2],
                                                ALU.subtract, ALU.mult))
                        link(pool.tensor_tensor(h2[:, qi, :], h2[:, qi, :], mod_row(b, 2), ALU.mult))
                        pool.tensor_tensor(h2[:, qi, :], h2[:, qi, :], mod_row(b, 1), ALU.add).then_inc(h2_made, 1)
                    if k == 3 and not last:
                        normalise(b + 1, link)
                pool.wait_ge(slots_made, nth(b, 1, 0))
                pool.wait_ge(h2_made, nth(b, NT, NT + 1))
                passed()
                for t in range(NT):
                    for c in range(2):
                        pool.indirect_dma_start(
                            out=rows_hbm[:, :],
                            out_offset=bass.IndirectOffsetOnAxis(ap=slot_now[:, c, t:t + 1], axis=0),
                            in_=h2[:, t, :], in_offset=None).then_inc(scattered, 16)
                pool.wait_ge(scattered, (b + 1) * (16 * 2 * NT))
                pool.sem_inc(indices_used, 1)

            def mod_row(b, n):
                return mod_rows[:, bass.ds(b, 1), n, :].rearrange("p a d -> p (a d)")

            with pool.Fori(0, B - 1) as b:
                batch(b, False)
            batch(B - 1, True)

            pool.wait_ge(y_slots_made, 1)
            for n in range(2):
                pool.wait_ge(y_out[n], 16 * ((TILES + 1 - n) // 2) + 16)
            for t in range(NTT):
                n = t % 8
                if t >= 8:
                    pool.wait_ge(o_made, t - 7)
                for c, (dst, arrived) in enumerate(((ya, ya_in), (yb, yb_in))):
                    pool.indirect_dma_start(
                        out=dst[:, n, :], out_offset=None, in_=y_hbm[:, :],
                        in_offset=bass.IndirectOffsetOnAxis(ap=slot_i[:, c, t:t + 1], axis=0)).then_inc(arrived[n], 16)

        @block.scalar
        def _(act):
            act.wait_ge(setup_pe, 1)
            act.activation(silu_c[:, :, :].rearrange("p c b -> p (c b)"), pmisc[:, 0:DC * B], ACT.Silu
                           ).then_inc(setup_act, 1)
            act.wait_ge(consts_made, 2)

            def batch(b, last):
                act.wait_ge(mod_now_made, nth(b, 1, 0))
                for t in range(0, NT, 2):
                    act.wait_ge(tp_full[0], nth(b, TP_HALF, t // 2))
                    for c in range(DC):
                        ins = act.activation(hT[:, c, t * P:(t + 1) * P], tp[0][:, c * P:(c + 1) * P], ACT.Identity,
                                             bias=mod_now[:, c:c + 1], scale=mod_now[:, DC + c:DC + c + 1])
                    ins.then_inc(tp_free[0], 1)
                act.wait_ge(sc_full[0], nth(b, SC_HALF, 0))
                act.copy(qT[:, 0, :], sc[0][:, :]).then_inc(sc_free[0], 1)
                act.wait_ge(sc_full[0], nth(b, SC_HALF, 1))
                act.copy(v_sb[:, 0:NT // 2, :].rearrange("p t d -> p (t d)"), sc[0][:, :]).then_inc(sc_free[0], 1)
                for k in STEPS:
                    if 0 <= k < NT:
                        for g, n in groups_of(k):
                            u = TP_AT[("p", k, g)]
                            act.wait_ge(tp_full[u % 2], nth(b, TP_HALF, u // 2))
                            act.copy(probT[:, k % 2, g * P:(g + n) * P], tp[u % 2][:, 0:n * P]
                                     ).then_inc(tp_free[u % 2], 1)
                    if 0 <= k + 1 < NT:
                        pos = k + 1
                        qi = ORDER[pos]
                        w = (NT - qi) * P
                        act.wait_ge(masked, nth(b, NT, pos))
                        act.activation(prob[:, pos % 2, 0:w], prob[:, pos % 2, 0:w], ACT.Exp,
                                       bias=negmax[:, pos:pos + 1], accum_out=rowsum[:, pos:pos + 1]
                                       ).then_inc(exp_made, 1)
                        if qi > 0:
                            act.activation(pm_rows[:, pos, 0:qi], negmax[:, pos:pos + 1].to_broadcast([P, qi]),
                                           ACT.Exp, bias=neg_col[:, :]).then_inc(pm_made, 1)
                    if 0 <= k - 3 < NT:
                        pos = k - 3
                        u = TP_AT[("h", pos)]
                        act.wait_ge(tp_full[u % 2], nth(b, TP_HALF, u // 2))
                        act.copy(h2T[:, pos % 2, :], tp[u % 2][:, 0:D]).then_inc(tp_free[u % 2], 1)
                for n in range(2):
                    act.wait_ge(routed_exp, nth(b, 2, n))
                    if n == 0:
                        flat = rt[0][:, :, :].rearrange("p t e -> p (t e)")
                    else:
                        flat = rs[2][:, :]
                    act.activation(flat, flat, ACT.Exp).then_inc(exp_routed, 1)

            with act.Fori(0, B - 1) as b:
                batch(b, False)
            batch(B - 1, True)

            def silu(t, par):
                act.wait_ge(gu_full, t + 1)
                act.activation(act_sb[:, par, :], sc[0][:, par * F:(par + 1) * F], ACT.Silu).then_inc(act_made, 1)

            def fused_out(t, par):
                act.wait_ge(fTp_full, t + 1)
                act.copy(fusedT[:, par, :], tp[1][:, :]).then_inc(fusedT_made, 1)

            silu(0, 0)
            silu(1, 1)
            fused_out(0, 0)
            with act.Fori(0, (TILES - 3) // 2) as i:
                for u in range(2):
                    silu(2 * i + 2 + u, u)
                    fused_out(2 * i + 1 + u, (1 + u) % 2)
            silu(TILES - 1, 0)
            fused_out(TILES - 2, 1)
            fused_out(TILES - 1, 0)

        @block.vector
        def _(dve):
            done = [0]

            def link(ins):
                done[0] += 1
                ins.then_inc(dve_done, 1)
                dve.wait_ge(dve_done, done[0])

            for s, n in ((tp_free[0], 1), (tp_free[1], 1), (x1_made, 4), (h2_made, 2), (x1_stored[0], 16),
                         (x1_stored[1], 16), (indices_used, 1), (y_out[0], 16), (y_out[1], 16)):
                dve.nop().then_inc(s, n)
            dve.wait_ge(setup_pe, 2)
            wT = hT
            link(dve.tensor_copy(wT[:, 0, :], sc[0][:, :]))
            dve.nop().then_inc(setup_dve, 1)
            dve.wait_ge(setup_pe, 3)
            dve.tensor_scalar(qk_sb[:, :, :].rearrange("p c d -> p (c d)"), po[:, :], float(D) ** -0.5, None, ALU.mult
                              ).then_inc(setup_dve, 1)
            silu_rows = probT[:, 0, :].rearrange("p (a m) -> p a m", m=P)
            dve.wait_ge(setup_act, 1)
            dve.tensor_copy(silu_rows, silu_c[:, :, :].rearrange("p c b -> p (c b)").unsqueeze(2).to_broadcast([P, DC * B, P])
                            ).then_inc(setup_dve, 1)
            dve.wait_ge(setup_pe, 4)
            cols = mod_cols[:, :, :].rearrange("p j b -> p (j b)")
            link(dve.tensor_copy(cols, pmisc[:, 0:2 * DC * B]))
            half = DC * B
            dve.tensor_scalar(cols[:, half:2 * half], cols[:, half:2 * half], 1.0, None, ALU.add).then_inc(dve_done, 1)
            done[0] += 1
            for b in range(B):
                buf = sc[(b + 1) % 2]
                dve.wait_ge(setup_pe, 5 + b)
                rows = mod_rows[:, b, :, :]
                link(dve.tensor_copy(rows.rearrange("p j d -> p (j d)"), buf[:, :]))
                dve.nop().then_inc(setup_dve, 1)
                link(dve.tensor_scalar(rows[:, 2, :], rows[:, 2, :], 1.0, None, ALU.add))
                for j in (0, 3):
                    sign = pen[:, 0:D]
                    link(dve.tensor_scalar(sign, rows[:, j, :], 0.0, 2.0, ALU.is_ge, ALU.mult))
                    link(dve.tensor_scalar(sign, sign, 1.0, None, ALU.subtract))
                    size = pen[:, D:2 * D]
                    link(dve.tensor_scalar(size, rows[:, j, :], -1.0, None, ALU.mult))
                    link(dve.tensor_tensor(size, rows[:, j, :], size, ALU.max))
                    link(dve.tensor_scalar(rows[:, j, :], size, 0.25, None, ALU.max))
                    link(dve.tensor_tensor(rows[:, j, :], rows[:, j, :], sign, ALU.mult))
            for s in (po_free, misc_free, sc_free[0], sc_free[1]):
                dve.nop().then_inc(s, 1)

            dve.wait_ge(x_in, 16)
            for t in range(NT):
                link(dve.bn_stats(stats[:, t, :], xb[:, t, :]))
            for t in range(NT):
                link(dve.bn_aggr(mv[:, t, :], stats[:, t, :]))
            dve.nop().then_inc(stats_made, 1)
            dve.wait_ge(consts_made, 2)

            def batch(b, last):
                at = [0]
                dve.sem_clear(dve_done)

                def link(ins):
                    at[0] += 1
                    ins.then_inc(dve_done, 1)
                    dve.wait_ge(dve_done, at[0])

                def counted(ins):
                    at[0] += 1
                    ins.then_inc(dve_done, 1)

                dve.tensor_copy(mod_now[:, :], mod_cols[:, :, bass.ds(b, 1)].rearrange("p j a -> p (j a)")
                                ).then_inc(mod_now_made, 1)
                dve.wait_ge(mod_now_made, nth(b, 1, 0))
                for t in range(1, NT, 2):
                    dve.wait_ge(tp_full[1], nth(b, TP_HALF, t // 2))
                    for c in range(DC):
                        ins = dve.tensor_scalar(hT[:, c, t * P:(t + 1) * P], tp[1][:, c * P:(c + 1) * P],
                                                mod_now[:, DC + c:DC + c + 1], mod_now[:, c:c + 1], ALU.mult, ALU.add)
                    ins.then_inc(tp_free[1], 1)
                dve.wait_ge(sc_full[1], nth(b, SC_HALF, 0))
                dve.tensor_copy(qT[:, 1, :], sc[1][:, :]).then_inc(sc_free[1], 1)
                dve.wait_ge(tp_free[0], b * TP_HALF + 5)
                dve.wait_ge(tp_free[1], b * TP_HALF + 5)
                dve.tensor_reduce(hsum[:, :, :].rearrange("p c t -> p (c t)"),
                                  hT[:, :, :].rearrange("p c (t s) -> p (c t) s", s=P), AX.X, ALU.add
                                  ).then_inc(hsum_made, 1)
                dve.wait_ge(sc_full[1], nth(b, SC_HALF, 1))
                dve.tensor_copy(v_sb[:, NT // 2:, :].rearrange("p t d -> p (t d)"), sc[1][:, :]).then_inc(sc_free[1], 1)
                dve.wait_ge(misc_full, nth(b, len(MISC_USES), MISC_AT["vsum"]))
                dve.tensor_copy(vsum[:, :], pmisc[0:NT, 0:D]).then_inc(misc_free, 1)

                for k in STEPS:
                    if 0 <= k + 1 < NT:
                        pos = k + 1
                        qi = ORDER[pos]
                        w = (NT - qi) * P
                        buf = sc[pos % 2]
                        dve.wait_ge(sc_full[pos % 2], nth(b, SC_HALF, 2 + pos // 2))
                        link(dve.tensor_tensor(buf[:, 0:P], buf[:, 0:P], upper[:, :], ALU.mult))
                        link(dve.tensor_scalar(pen[:, 0:w], buf[:, 0:w], 0.0, MASK_NEG, ALU.is_equal, ALU.mult))
                        if pos >= 2:
                            u = TP_AT[("p", pos - 2, groups_of(pos - 2)[-1][0])]
                            dve.wait_ge(tp_full[u % 2], nth(b, TP_HALF, u // 2))
                        dve.tensor_tensor(prob[:, pos % 2, 0:w], buf[:, 0:w], pen[:, 0:w], ALU.add
                                          ).then_inc(sc_free[pos % 2], 1)
                        dve.wait_ge(sc_free[pos % 2], b * SC_HALF + (2 + pos // 2 + 2))
                        if qi > 0:
                            link(dve.tensor_reduce(negmax[:, pos:pos + 1], prob[:, pos % 2, 0:w], AX.X, ALU.max, negate=True))
                            dve.tensor_scalar(negmax[:, pos:pos + 1], negmax[:, pos:pos + 1], -MASK_NEG, None, ALU.min
                                              ).then_inc(masked, 1)
                        else:
                            dve.tensor_reduce(negmax[:, pos:pos + 1], prob[:, pos % 2, 0:w], AX.X, ALU.max, negate=True
                                              ).then_inc(masked, 1)
                    if 0 <= k < NT:
                        qi = ORDER[k]
                        dve.wait_ge(exp_made, nth(b, NT, k))
                        if qi > 0:
                            npm = sum(1 for q in ORDER[:k] if q > 0)
                            dve.wait_ge(pm_made, nth(b, NT - 1, npm))
                            link(dve.scalar_tensor_tensor(out=rowsum[:, k:k + 1], in0=pm_rows[:, k, 0:1],
                                                          scalar=float(P * qi), in1=rowsum[:, k:k + 1],
                                                          op0=ALU.mult, op1=ALU.add))
                        link(dve.reciprocal(rinv[:, k:k + 1], rowsum[:, k:k + 1]))
                        if qi > 0:
                            m = MISC_AT[("pm", k)]
                            dve.wait_ge(misc_full, nth(b, len(MISC_USES), m))
                            dve.tensor_copy(pmT[:, k % 2, :], pmisc[0:NT, 0:P]).then_inc(misc_free, 1)
                    if 0 <= k - 1 < NT:
                        pos = k - 1
                        qi = ORDER[pos]
                        dve.wait_ge(po_full, nth(b, NT, pos))
                        dve.wait_ge(h2_made, nth(b, NT, pos))
                        dve.wait_ge(x1_stored[pos % 2], b * (8 * NT) + 16 * (pos // 2 + 1))
                        dve.scalar_tensor_tensor(out=x1[:, pos % 2, :], in0=po[:, 0:D], scalar=rinv[:, pos:pos + 1],
                                                 in1=mod_rows[:, bass.ds(b, 1), 0, :].rearrange("p a d -> p (a d)"),
                                                 op0=ALU.mult, op1=ALU.mult).then_inc(po_free, 1)
                        dve.wait_ge(po_free, b * NT + (pos + 2))
                        dve.wait_ge(xr_in[pos % 4], b * 32 + 16 * (pos // 4 + 1))
                        dve.tensor_tensor(x1[:, pos % 2, :], x1[:, pos % 2, :], xr[:, pos % 4, :], ALU.add
                                          ).then_inc(x1_made, 1)
                        dve.wait_ge(x1_made, b * NT + (pos + 5))
                        link(dve.bn_stats(stats2[:, :], x1[:, pos % 2, :]))
                        dve.bn_aggr(mv2[:, pos % 2, :], stats2[:, :]).then_inc(mv2_made, 1)
                    if 0 <= k - 4 < NT:
                        pos = k - 4
                        dve.wait_ge(misc_full, nth(b, len(MISC_USES), MISC_AT[("lg", pos)]))
                        dve.tensor_copy(lg[:, ORDER[pos], :], pmisc[:, 0:E]).then_inc(misc_free, 1)
                    if k == 2 and not last:
                        dve.wait_ge(x_in, b * 16 + 32)
                        for t in range(NT):
                            link(dve.bn_stats(stats[:, t, :], xb[:, t, :]))
                        for t in range(NT):
                            ins = dve.bn_aggr(mv[:, t, :], stats[:, t, :])
                            if t < NT - 1:
                                counted(ins)
                        ins.then_inc(stats_made, 1)

                route(b, link)

            def route(b, link):
                p3, t3, q3 = (r[:, :, :] for r in rt)
                s0, s1, s2, s3 = (r[:, :] for r in rs)

                def wide(s):
                    return s.unsqueeze(2).to_broadcast([P, NT, E])

                dve.wait_ge(misc_free, b * len(MISC_USES) + (MISC_AT[("lg", NT - 1)] + 2))
                link(dve.tensor_reduce(s0, lg[:, :, :], AX.X, ALU.max))
                dve.tensor_tensor(p3, lg[:, :, :], wide(s0), ALU.subtract).then_inc(routed_exp, 1)
                dve.wait_ge(exp_routed, nth(b, 2, 0))
                link(dve.tensor_reduce(s0, p3, AX.X, ALU.add))
                link(dve.reciprocal(s1, s0))
                link(dve.tensor_tensor(p3, p3, wide(s1), ALU.mult))
                rank3 = choice_rank[:, :].unsqueeze(1).to_broadcast([P, NT, E])
                region3 = region[:, :].unsqueeze(1).to_broadcast([P, NT, E])
                now = bass.ds(b * NT, NT)
                for c, top in ((0, s0), (1, s1)):
                    one_hot = pick[:, c, now, :]
                    link(dve.tensor_reduce(top, p3, AX.X, ALU.max))
                    link(dve.tensor_tensor(t3, p3, wide(top), ALU.is_equal))
                    link(dve.tensor_tensor(t3, t3, rank3, ALU.mult))
                    link(dve.tensor_reduce(s3, t3, AX.X, ALU.max))
                    link(dve.tensor_tensor(one_hot, t3, wide(s3), ALU.is_equal))
                    if c == 0:
                        link(dve.scalar_tensor_tensor(out=p3, in0=one_hot, scalar=-2.0, in1=p3, op0=ALU.mult, op1=ALU.add))
                link(dve.tensor_tensor(chosen[:, :, :], pick[:, 0, now, :], pick[:, 1, now, :], ALU.add))
                for t in range(NT):
                    ins = dve.tensor_tensor(seen[:, t + 1, :], seen[:, t, :], chosen[:, t, :], ALU.add)
                    if t < NT - 1:
                        link(ins)
                ins.then_inc(chosen_made, 1)
                dve.tensor_tensor(s2, s1, s0, ALU.subtract).then_inc(routed_exp, 1)
                dve.wait_ge(exp_routed, nth(b, 2, 1))
                link(dve.tensor_scalar(s3, s2, 1.0, None, ALU.add))
                link(dve.reciprocal(weight[:, 0, now], s3))
                link(dve.tensor_tensor(weight[:, 1, now], s2, weight[:, 0, now], ALU.mult))
                dve.wait_ge(misc_full, nth(b, len(MISC_USES), MISC_AT["rank"]))
                dve.tensor_tensor(t3, pmisc[:, 0:NT * E].rearrange("p (t e) -> p t e", e=E), region3, ALU.add
                                  ).then_inc(misc_free, 1)
                dve.wait_ge(misc_free, b * len(MISC_USES) + (MISC_AT["rank"] + 2))
                dve.wait_ge(indices_used, nth(b, 1, 0))
                for c in range(2):
                    link(dve.tensor_tensor(q3, t3, pick[:, c, now, :], ALU.mult))
                    link(dve.tensor_reduce(slot[:, c, now], q3, AX.X, ALU.add))
                    ins = dve.tensor_copy(slot_now[:, c, :], slot[:, c, now])
                    if c == 0:
                        link(ins)
                ins.then_inc(slots_made, 1)
                link(dve.tensor_copy(seen[:, 0, :], seen[:, NT, :]))

            with dve.Fori(0, B - 1) as b:
                batch(b, False)
            batch(B - 1, True)

            dve.sem_clear(dve_done)
            done[0] = 0
            dve.wait_ge(misc_full, B * len(MISC_USES) + 1)
            link(dve.tensor_copy(count[:, :], pmisc[:, 0:E]))
            g3 = grid[:, 0:E * NTT].rearrange("p (e m) -> p e m", e=E)
            link(dve.tensor_tensor(g3, count[:, :].unsqueeze(2).to_broadcast([P, E, NTT]),
                                   steps32[:, :].unsqueeze(1).to_broadcast([P, E, NTT]), ALU.is_gt))
            link(dve.tensor_reduce(tiles_of[:, :], g3, AX.X, ALU.add))
            g8 = grid[:, 0:E * E].rearrange("p (a b) -> p a b", a=E)
            link(dve.tensor_tensor(g8, lower8[:, :, :], tiles_of[:, :].unsqueeze(1).to_broadcast([P, E, E]), ALU.mult))
            link(dve.tensor_reduce(end_of[:, :], g8, AX.X, ALU.add))
            ge = grid[0:1, :].rearrange("p (t e) -> p t e", e=E)
            gs = grid2[0:1, :].rearrange("p (t e) -> p t e", e=E)
            wide_t = tile_no[:, :].unsqueeze(2).to_broadcast([1, TILES, E])
            link(dve.tensor_tensor(ge, wide_t, end_of[0:1, :].unsqueeze(1).to_broadcast([1, TILES, E]), ALU.is_ge))
            link(dve.tensor_tensor(gs, ge, tiles_of[0:1, :].unsqueeze(1).to_broadcast([1, TILES, E]), ALU.mult))
            link(dve.tensor_reduce(tile_exp[:, :], ge, AX.X, ALU.add))
            link(dve.tensor_reduce(tile_row[:, :], gs, AX.X, ALU.add))
            link(dve.tensor_tensor(tile_row[:, :], tile_no[:, :], tile_row[:, :], ALU.subtract))
            link(dve.tensor_scalar(tile_row[:, :], tile_row[:, :], float(P), None, ALU.mult))
            link(dve.scalar_tensor_tensor(out=tile_row[:, :], in0=tile_exp[:, :], scalar=float(REG), in1=tile_row[:, :],
                                          op0=ALU.mult, op1=ALU.add))
            link(dve.tensor_scalar(tile_row[:, :], tile_row[:, :], float(DUMMY), None, ALU.min))
            link(dve.tensor_copy(tile_row_i[:, :], tile_row[:, :]))
            link(dve.tensor_scalar(tile_exp[:, :], tile_exp[:, :], float(E - 1), None, ALU.min))
            dve.tensor_copy(tile_exp_i[:, :], tile_exp[:, :]).then_inc(table_made, 1)
            link(dve.tensor_tensor(start_delta[0:1, :], count[0:1, :], region[0:1, :], ALU.add))
            dve.tensor_copy(pad_i[:, :], start_delta[0:1, :]).then_inc(table_made, 1)
            dve.wait_ge(table_made, 2)
            link(dve.tensor_tensor(start_delta[:, :], end_of[:, :], tiles_of[:, :], ALU.subtract))
            link(dve.tensor_scalar(start_delta[:, :], start_delta[:, :], float(P), None, ALU.mult))
            link(dve.tensor_tensor(start_delta[:, :], start_delta[:, :], region[:, :], ALU.subtract))
            gt = grid[:, 0:NTT * E].rearrange("p (t e) -> p t e", e=E)
            for c in range(2):
                link(dve.tensor_tensor(gt, pick[:, c, :, :], start_delta[:, :].unsqueeze(1).to_broadcast([P, NTT, E]),
                                       ALU.mult))
                link(dve.tensor_reduce(grid2[:, 0:NTT], gt, AX.X, ALU.add))
                link(dve.tensor_tensor(slot[:, c, :], slot[:, c, :], grid2[:, 0:NTT], ALU.add))
                link(dve.tensor_copy(slot_i[:, c, :], slot[:, c, :]))
            dve.nop().then_inc(y_slots_made, 1)

            def rows_out(t, par):
                dve.wait_ge(hTp_full, t + 1)
                dve.tensor_copy(hinT[:, par, :], tp[0][:, 0:D]).then_inc(hinT_made, 1)

            def product(t, par):
                dve.wait_ge(act_made, t + 1)
                dve.tensor_tensor(fused[:, par, :], act_sb[:, par, :], sc[1][:, par * F:(par + 1) * F], ALU.mult
                                  ).then_inc(fused_made, 1)

            def y_to_sbuf(t, par, stored):
                dve.wait_ge(y_full, t + 1)
                dve.wait_ge(y_out[par], stored)
                dve.tensor_copy(y_sb[:, par, :], (po if par == 0 else pmisc)[:, 0:D]).then_inc(y_made, 1)

            rows_out(0, 0)
            rows_out(1, 1)
            product(0, 0)
            product(1, 1)
            rows_out(2, 0)
            with dve.Fori(0, (TILES - 3) // 2) as i:
                for u in range(2):
                    product(2 * i + 2 + u, u)
                    rows_out(2 * i + 3 + u, (1 + u) % 2)
                    y_to_sbuf(2 * i + u, u, 16 * i + 16)
            product(TILES - 1, 0)
            for t in range(TILES - 3, TILES):
                y_to_sbuf(t, t % 2, 16 * (t // 2) + 16)

            for t in range(NTT):
                n, b = t % 8, t // NT
                dve.wait_ge(ya_in[n], 16 * (t // 8 + 1))
                link(dve.tensor_scalar(ya[:, n, :], ya[:, n, :], weight[:, 0, t:t + 1], None, ALU.mult))
                dve.wait_ge(yb_in[n], 16 * (t // 8 + 1))
                link(dve.scalar_tensor_tensor(out=ya[:, n, :], in0=yb[:, n, :], scalar=weight[:, 1, t:t + 1],
                                              in1=ya[:, n, :], op0=ALU.mult, op1=ALU.add))
                link(dve.tensor_tensor(ya[:, n, :], ya[:, n, :], mod_rows[:, b, 3, :], ALU.mult))
                dve.wait_ge(xc_in[n], 16 * (t // 8 + 1))
                if t >= 8:
                    dve.wait_ge(out_done[n], 16 * (t // 8))
                dve.tensor_tensor(oc[:, n, :], ya[:, n, :], xc[:, n, :], ALU.add).then_inc(o_made, 1)

        @block.tensor
        def _(pe):
            pe.wait_ge(consts_made, 2)
            pe.wait_ge(cond_in, 16)
            for c in range(DC):
                mm = pe.transpose(pmisc[:, c * B:(c + 1) * B], prob[0:B, 0, c * P:(c + 1) * P], ident[0:B, 0:B])
            mm.then_inc(setup_pe, 1)
            pe.wait_ge(attn_in, 16)
            for j in range(2):
                for f in range(DC):
                    for c in range(DC):
                        o = (j * DC + f) * D + c * P
                        mm = pe.transpose(sc[0][:, o:o + P], attn_sb[:, c, j * D + f * P:j * D + (f + 1) * P], ident[:, :])
            mm.then_inc(setup_pe, 1)
            pe.wait_ge(setup_dve, 1)
            for i in range(DC):
                for f in range(DC):
                    mm = pe.matmul(po[:, i * D:(i + 1) * D], hT[:, 0, f * D + i * P:f * D + (i + 1) * P],
                                   hT[:, 0, (DC + f) * D:(DC + f + 1) * D], start=(f == 0), stop=(f == DC - 1))
            mm.then_inc(setup_pe, 1)
            pe.wait_ge(setup_act, 1)
            pe.wait_ge(wmod_in, 16)
            wmod_sb = qv[:, 0:DC * 6 * D].rearrange("p (c n) -> p c n", c=DC)
            for j in range(2 * DC):
                for c in range(DC):
                    mm = pe.matmul(pmisc[:, j * B:(j + 1) * B], wmod_sb[:, c, j * P:(j + 1) * P], silu_c[:, c, :],
                                   start=(c == 0), stop=(c == DC - 1))
            mm.then_inc(setup_pe, 1)
            pe.wait_ge(setup_dve, 3)
            for b in range(B):
                buf = sc[(b + 1) % 2]
                if b >= 2:
                    pe.wait_ge(setup_dve, 3 + b - 1)
                for half in range(2):
                    for c in range(DC):
                        mm = pe.matmul(buf[:, half * 512:(half + 1) * 512],
                                       probT[:, 0, (c * B + b) * P:(c * B + b + 1) * P],
                                       wmod_sb[:, c, 2 * D + half * 512:2 * D + (half + 1) * 512],
                                       start=(c == 0), stop=(c == DC - 1))
                mm.then_inc(setup_pe, 1)
            pe.wait_ge(router_in, 16)

            def batch(b, last):
                for t in range(NT):
                    pe.wait_ge(xn_made, nth(b, NT, t))
                    pe.wait_ge(tp_free[t % 2], nth(b, TP_HALF, t // 2))
                    for c in range(DC):
                        mm = pe.transpose(tp[t % 2][:, c * P:(c + 1) * P], xb[:, t, c * P:(c + 1) * P], ident[:, :])
                    mm.then_inc(tp_full[t % 2], 1)
                pe.wait_ge(tp_free[0], b * TP_HALF + 5)
                pe.wait_ge(tp_free[1], b * TP_HALF + 5)
                for f in range(DC):
                    pe.wait_ge(sc_free[f], nth(b, SC_HALF, 0))
                    for half in range(2):
                        for c in range(DC):
                            mm = pe.matmul(sc[f][:, half * 512:(half + 1) * 512], qk_sb[:, c, f * P:(f + 1) * P],
                                           hT[:, c, half * 512:(half + 1) * 512], start=(c == 0), stop=(c == DC - 1))
                    mm.then_inc(sc_full[f], 1)
                for half in range(2):
                    pe.wait_ge(sc_free[half], nth(b, SC_HALF, 1))
                    for i in range(NT // 2):
                        t = half * NT // 2 + i
                        for c in range(DC):
                            mm = pe.matmul(sc[half][:, i * D:(i + 1) * D], hT[:, c, t * P:(t + 1) * P],
                                           attn_sb[:, c, 2 * D:3 * D], start=(c == 0), stop=(c == DC - 1))
                    mm.then_inc(sc_full[half], 1)
                pe.wait_ge(hsum_made, nth(b, 1, 0))
                pe.wait_ge(misc_free, nth(b, len(MISC_USES), MISC_AT["vsum"]))
                for c in range(DC):
                    mm = pe.matmul(pmisc[0:NT, 0:D], hsum[:, c, :], attn_sb[:, c, 2 * D:3 * D],
                                   start=(c == 0), stop=(c == DC - 1))
                mm.then_inc(misc_full, 1)
                for k in STEPS:
                    if 0 <= k + 1 < NT:
                        pos = k + 1
                        qi = ORDER[pos]
                        w = (NT - qi) * P
                        pe.wait_ge(sc_free[pos % 2], nth(b, SC_HALF, 2 + pos // 2))
                        for o in range(0, w, 512):
                            n = min(512, w - o)
                            for c in range(DC):
                                mm = pe.matmul(sc[pos % 2][:, o:o + n], qT[:, c, qi * P:(qi + 1) * P],
                                               hT[:, c, qi * P + o:qi * P + o + n], start=(c == 0), stop=(c == DC - 1))
                        mm.then_inc(sc_full[pos % 2], 1)
                    if 0 <= k < NT:
                        qi = ORDER[k]
                        pe.wait_ge(exp_made, nth(b, NT, k))
                        for g, n in groups_of(k):
                            u = TP_AT[("p", k, g)]
                            pe.wait_ge(tp_free[u % 2], nth(b, TP_HALF, u // 2))
                            for i in range(n):
                                mm = pe.transpose(tp[u % 2][:, i * P:(i + 1) * P],
                                                  prob[:, k % 2, (g + i) * P:(g + i + 1) * P], ident[:, :])
                            mm.then_inc(tp_full[u % 2], 1)
                        if qi > 0:
                            npm = sum(1 for q in ORDER[:k] if q > 0)
                            pe.wait_ge(pm_made, nth(b, NT - 1, npm))
                            pe.wait_ge(misc_free, nth(b, len(MISC_USES), MISC_AT[("pm", k)]))
                            pe.transpose(pmisc[0:NT, 0:P], pm_rows[:, k, :], ident[:, :]).then_inc(misc_full, 1)
                    if 0 <= k - 1 < NT:
                        pos = k - 1
                        qi = ORDER[pos]
                        pe.wait_ge(po_free, nth(b, NT, pos))
                        for g, n in groups_of(pos):
                            u = TP_AT[("p", pos, g)]
                            pe.wait_ge(tp_free[u % 2], b * TP_HALF + (u // 2 + 2))
                            for i in range(n):
                                j = g + i
                                mm = pe.matmul(po[:, 0:D], probT[:, pos % 2, j * P:(j + 1) * P], v_sb[:, qi + j, :],
                                               start=(j == 0), stop=(j == NT - 1 - qi and qi == 0))
                        if qi > 0:
                            pe.wait_ge(misc_free, b * len(MISC_USES) + (MISC_AT[("pm", pos)] + 2))
                            mm = pe.matmul(po[:, 0:D], pmT[:, pos % 2, :], vsum[:, :], start=False, stop=True)
                        mm.then_inc(po_full, 1)
                    if 0 <= k - 3 < NT:
                        pos = k - 3
                        u = TP_AT[("h", pos)]
                        pe.wait_ge(h2_made, nth(b, NT, pos + 2))
                        pe.wait_ge(tp_free[u % 2], nth(b, TP_HALF, u // 2))
                        for c in range(DC):
                            mm = pe.transpose(tp[u % 2][:, c * P:(c + 1) * P], h2[:, ORDER[pos], c * P:(c + 1) * P], ident[:, :])
                        mm.then_inc(tp_full[u % 2], 1)
                    if 0 <= k - 4 < NT:
                        pos = k - 4
                        u = TP_AT[("h", pos)]
                        pe.wait_ge(tp_free[u % 2], b * TP_HALF + (u // 2 + 2))
                        pe.wait_ge(misc_free, nth(b, len(MISC_USES), MISC_AT[("lg", pos)]))
                        for c in range(DC):
                            mm = pe.matmul(pmisc[:, 0:E], h2T[:, pos % 2, c * P:(c + 1) * P], router_sb[:, c, :],
                                           start=(c == 0), stop=(c == DC - 1))
                        mm.then_inc(misc_full, 1)
                pe.wait_ge(chosen_made, nth(b, 1, 0))
                pe.wait_ge(misc_free, nth(b, len(MISC_USES), MISC_AT["rank"]))
                pe.matmul(pmisc[:, 0:NT * E], before[:, :], chosen[:, :, :].rearrange("p t e -> p (t e)"),
                          start=True, stop=False)
                pe.matmul(pmisc[:, 0:NT * E], ones[:, :], seen[:, 0:NT, :].rearrange("p t e -> p (t e)"),
                          start=False, stop=True).then_inc(misc_full, 1)

            with pe.Fori(0, B - 1) as b:
                batch(b, False)
            batch(B - 1, True)
            pe.wait_ge(misc_free, B * len(MISC_USES) + 1)
            pe.matmul(pmisc[:, 0:E], ones[:, :], seen[:, NT, :], start=True, stop=True).then_inc(misc_full, 1)

            pe.wait_ge(table_made, 2)
            pe.wait_ge(expert_in, 16 * 3 * E)

            def expert_of(t):
                return pe.value_load(tile_exp_i[0:1, bass.ds(t, 1)], min_val=0, max_val=E - 1)

            def rows_t(t, par, arrived, first=False):
                pe.wait_ge(hin_in[par], arrived)
                if not first:
                    pe.wait_ge(hinT_made, t)
                for c in range(DC):
                    mm = pe.transpose(tp[0][:, c * P:(c + 1) * P], hin[:, par, c * P:(c + 1) * P], ident[:, :])
                mm.then_inc(hTp_full, 1)

            def gate_up(t, par, early=False):
                e = expert_of(t)
                pe.wait_ge(hinT_made, t + 1)
                if not early:
                    pe.wait_ge(fused_made, t - 1)
                for w, buf in ((gate_sb, sc[0]), (up_sb, sc[1])):
                    for c in range(DC):
                        mm = pe.matmul(buf[:, par * F:(par + 1) * F], hinT[:, par, c * P:(c + 1) * P],
                                       w[:, bass.ds(e, 1), c, :].rearrange("p a f -> p (a f)"),
                                       start=(c == 0), stop=(c == DC - 1))
                mm.then_inc(gu_full, 1)

            def fused_t(t, par, first=False):
                pe.wait_ge(fused_made, t + 1)
                if not first:
                    pe.wait_ge(fusedT_made, t)
                for f in range(FC):
                    mm = pe.transpose(tp[1][:, f * P:(f + 1) * P], fused[:, par, f * P:(f + 1) * P], ident[:, :])
                mm.then_inc(fTp_full, 1)

            def down(t, par, early=False):
                e = expert_of(t)
                pe.wait_ge(fusedT_made, t + 1)
                if not early:
                    pe.wait_ge(y_made, t - 1)
                for f in range(FC):
                    mm = pe.matmul((po if par == 0 else pmisc)[:, 0:D], fusedT[:, par, f * P:(f + 1) * P],
                                   down_sb[:, bass.ds(e, 1), f, :].rearrange("p a d -> p (a d)"),
                                   start=(f == 0), stop=(f == FC - 1))
                mm.then_inc(y_full, 1)

            rows_t(0, 0, 16, first=True)
            rows_t(1, 1, 16)
            gate_up(0, 0, early=True)
            gate_up(1, 1, early=True)
            fused_t(0, 0, first=True)
            rows_t(2, 0, 32)
            gate_up(2, 0)
            fused_t(1, 1)
            rows_t(3, 1, 32)
            down(0, 0, early=True)
            gate_up(3, 1)
            fused_t(2, 0)
            rows_t(4, 0, 48)
            down(1, 1, early=True)
            with pe.Fori(1, (TILES - 3) // 2) as i:
                for u in range(2):
                    gate_up(2 * i + 2 + u, u)
                    fused_t(2 * i + 1 + u, (1 + u) % 2)
                    rows_t(2 * i + 3 + u, (1 + u) % 2, 16 * i + (32 + 16 * u))
                    down(2 * i + u, u)
            gate_up(TILES - 1, 0)
            fused_t(TILES - 2, 1)
            down(TILES - 3, 0)
            fused_t(TILES - 1, 0)
            down(TILES - 2, 1)
            down(TILES - 1, 0)


_INS = ['L0_attn_x', 'L0_attn_W', 'L0_ffn_router_kernel_DE', 'L0_ffn_kernel_gating_EDF', 'L0_ffn_kernel_up_EDF',
        'L0_ffn_kernel_down_EFD', 'L0_c', 'L0_wmod']
_OUTS = [((B, S, D), 'float32')]


def kernel(**inputs):
    import numpy as _np
    import concourse.bacc as _bacc
    from concourse import mybir as _mybir
    from concourse.bass_utils import run_bass_kernel_spmd as _run

    nc = _bacc.Bacc("TRN2", target_bir_lowering=False, num_devices=1)
    arrays, args = {}, []
    for name in _INS:
        a = _np.ascontiguousarray(inputs[name])
        arrays[f"in_{name}_dram"] = a
        args.append(nc.dram_tensor(f"in_{name}_dram", a.shape, _mybir.dt.from_np(a.dtype), kind="ExternalInput").ap())
    for i, (shape, dtype) in enumerate(_OUTS):
        dt = _mybir.dt.from_np(_np.dtype(dtype))
        args.append(nc.dram_tensor(f"out_{i}_dram", shape, dt, kind="ExternalOutput").ap())
    build(nc, *args)
    r = _run(nc, [arrays], core_ids=[0])
    got = tuple(r.results[0][f"out_{i}_dram"] for i in range(len(_OUTS)))
    return got[0]
```

```python
from contextlib import ExitStack

import concourse.bass as bass
from concourse import mybir

fp32 = mybir.dt.float32
bf16 = mybir.dt.bfloat16
i32 = mybir.dt.int32
ALU = mybir.AluOpType
ACT = mybir.ActivationFunctionType
AX = mybir.AxisListType

P = 128
B, S, D = 4, 1024, 256
E, F = 8, 512
DC, FC = D // P, F // P
NT = S // P
HALF = S // 2
TOK = B * S
NTT = TOK // P
MASK_NEG = -9000000000000000.0
LOWEST = -3.4028234663852886e38
EPS = 1e-5
REG = TOK + P
DUMMY = E * REG
TILES = 2 * TOK // P + E - 1
ROW = D + 3
UN = 4
LOOPS = (TILES - 3) // UN
assert 1 + LOOPS * UN == TILES - 2

ORDER = [0, 7, 1, 6, 2, 5, 3, 4]
assert sorted(ORDER) == list(range(NT))
GROUP = 4
TAIL = [(5, 4), (6, 5), (7, 6), (None, 7)]


def groups_of(pos):
    n = NT - ORDER[pos]
    return [(g, min(GROUP, n - g)) for g in range(0, n, GROUP)]


class Uses:

    def __init__(self, own, tail, buffers):
        self.first, self.later, self.n = own, tail + own, buffers
        assert len(self.later) % buffers == 0

    def at(self, it, use, tail=False):
        if isinstance(it, int) and it == 0:
            k, rounds = self.first.index(use), 0
        else:
            k, rounds = len(self.first) + self.later.index(use), (it - 1) * (len(self.later) // self.n)
        return k % self.n, k // self.n, rounds

    def buf(self, it, use):
        return self.at(it, use)[0]

    def full(self, it, use):
        _, k, rounds = self.at(it, use)
        return rounds + (k + 1)

    def read(self, it, use):
        _, k, rounds = self.at(it, use)
        return rounds + (k + 2)


def main_uses():
    tp, misc = [("v", i) for i in range(NT // 2)], ["vsum"]
    for k in range(NT):
        tp += [("p", k, g) for g, _ in groups_of(k)]
        if ORDER[k] > 0:
            misc.append(("pm", k))
        if k >= 3:
            tp.append(("h", k - 3))
        if k >= 4:
            misc.append(("lg", k - 4))
    return tp, misc


TP_MAIN, MISC_MAIN = main_uses()
TP_TAIL = [("h", h) for h, _ in TAIL if h is not None]
MISC_TAIL = [("lg", n) for _, n in TAIL] + ["rank"]
TPU = Uses(TP_MAIN, TP_TAIL, 2)
MISCU = Uses(MISC_MAIN, MISC_TAIL, 1)
SC_USES = 3 + NT // 2


def nth(batch, per_batch, k):
    return batch * per_batch + (k + 1)


def build(nc, x, attn_w, router, w_gate, w_up, w_down, cond, w_mod, out):
    ctx = ExitStack()
    with ctx:
        def sb(name, shape, dt=fp32):
            return ctx.enter_context(nc.sbuf_tensor(name, shape, dt))

        def pb(name, shape):
            return ctx.enter_context(nc.psum_tensor(name, shape, fp32))

        def sem(name):
            return ctx.enter_context(nc.semaphore(name))

        rows_hbm = nc.dram_tensor("rows_hbm", [E * REG + P, ROW], fp32, kind="Internal").ap()
        sum_hbm = nc.dram_tensor("sum_hbm", [TOK + P, D], fp32, kind="Internal").ap()
        mod_hbm = nc.dram_tensor("mod_hbm", [B, 3 * D], fp32, kind="Internal").ap()
        gb_hbm = nc.dram_tensor("gb_hbm", [B, D], fp32, kind="Internal").ap()

        gate_sb = sb("gate_sb", [P, E, DC, F])
        up_sb = sb("up_sb", [P, E, DC, F])
        down_sb = sb("down_sb", [P, E, FC, D])

        ident = sb("ident", [P, P])
        upper = sb("upper", [P, P])
        before = sb("before", [P, P], bf16)
        ones = sb("ones", [P, P], bf16)
        neg_col = sb("neg_col", [P, 1])
        pad_row = sb("pad_row", [P, ROW])
        minus_half = sb("minus_half", [P, NT])
        region = sb("region", [P, E])
        choice_rank = sb("choice_rank", [P, E])
        int_tmp = sb("int_tmp", [P, P], i32)
        token_of = sb("token_of", [P, NTT, 2])

        attn_sb = sb("attn_sb", [P, DC, 3 * D])
        qk_sb = sb("qk_sb", [P, DC, D])
        router_sb = sb("router_sb", [P, DC, E])
        mod_rows = sb("mod_rows", [P, B, 3, D])
        mod_flat = sb("mod_flat", [B, 4, D])
        mod_cols = sb("mod_cols", [P, 2 * DC, B])
        mod_now = sb("mod_now", [P, 2 * DC])
        silu_c = sb("silu_c", [P, DC, B])
        xb = sb("xb", [P, NT, D])
        hT = sb("hT", [P, DC, S])
        qv = sb("qv", [P, DC * S + NT * D])
        qT = qv[:, 0:DC * S].rearrange("p (c s) -> p c s", c=DC)
        v_sb = qv[:, DC * S:].rearrange("p (t d) -> p t d", t=NT)
        pen = sb("pen", [P, S])
        prob = sb("prob", [P, 2, S])
        probT = sb("probT", [P, 2, S])
        xr = sb("xr", [P, 4, D])
        x1 = sb("x1", [P, 2, D])
        h2 = sb("h2", [P, NT, ROW])
        h2T = sb("h2T", [P, 2, D])
        hsum = sb("hsum", [P, DC, NT])
        vsum = sb("vsum", [NT, D])
        stats = sb("stats", [P, NT, 6])
        mv = sb("mv", [P, NT, 2])
        veps = sb("veps", [P, NT])
        rstd = sb("rstd", [P, NT])
        shift = sb("shift", [P, NT])
        stats2 = sb("stats2", [P, 6])
        mv2 = sb("mv2", [P, 2, 2])
        veps2 = sb("veps2", [P, 2])
        rstd2 = sb("rstd2", [P, 2])
        shift2 = sb("shift2", [P, 2])
        rowmax = sb("rowmax", [P, NT])
        negmax = sb("negmax", [P, NT])
        rowsum = sb("rowsum", [P, NT])
        rinv = sb("rinv", [P, NT])
        pm_rows = sb("pm_rows", [P, NT, NT])
        pmT = sb("pmT", [NT, 2, P])

        lg = sb("lg", [P, NT, E])
        rt = [sb(f"rt{n}", [P, NT, E]) for n in range(3)]
        rs = [sb(f"rs{n}", [P, NT]) for n in range(4)]
        pick = sb("pick", [P, 2, NT, E])
        slot = sb("slot", [P, NT])
        extra = sb("extra", [P, 2, NT, 3])
        slot_i = sb("slot_i", [P, 2, NT], i32)
        chosen = sb("chosen", [P, NT, E], bf16)
        seen = sb("seen", [P, NT + 1, E], bf16)

        count = sb("count", [P, E])
        tiles_of = sb("tiles_of", [P, E])
        end_of = sb("end_of", [P, E])
        pad_at = sb("pad_at", [1, E])
        steps32 = sb("steps32", [P, NTT])
        lower8 = sb("lower8", [P, E, E])
        tile_no = sb("tile_no", [1, TILES])
        tile_exp = sb("tile_exp", [1, TILES])
        tile_row = sb("tile_row", [1, TILES])
        tile_exp_i = sb("tile_exp_i", [1, TILES], i32)
        tile_row_i = sb("tile_row_i", [1, TILES], i32)
        pad_i = sb("pad_i", [1, E], i32)

        hin = xb[:, 0:5, :].rearrange("p t d -> p (t d)")[:, 0:UN * ROW].rearrange("p (r d) -> p r d", r=UN)
        hinT = hT[:, 0, 0:2 * D].rearrange("p (r d) -> p r d", r=2)
        act_sb = prob[:, 0, :].rearrange("p (r f) -> p r f", r=2)
        fused = prob[:, 1, :].rearrange("p (r f) -> p r f", r=2)
        fusedT = probT[:, 0, :].rearrange("p (r f) -> p r f", r=2)
        y_sb = xr
        row_weight = sb("row_weight", [P, UN, 1])
        place_i = sb("place_i", [P, UN, 2], i32)
        gb_rows = hT[:, 1, :].rearrange("p (n d) -> p n d", n=UN)
        grid = qv[:, 0:E * TILES]
        grid2 = pen[:, 0:E * TILES]
        tp = [pb(f"tp{n}", [P, 512]) for n in range(2)]
        sc = [pb(f"sc{n}", [P, 1024]) for n in range(2)]
        po = pb("po", [P, 512])
        pmisc = pb("pmisc", [P, 512])

        attn_in, router_in, cond_in, wmod_in = sem("attn_in"), sem("router_in"), sem("cond_in"), sem("wmod_in")
        expert_in, pads_out, mod_out, mod_in = sem("expert_in"), sem("pads_out"), sem("mod_out"), sem("mod_in")
        consts_made, pool_done, dve_done = sem("consts_made"), sem("pool_done"), sem("dve_done")
        pool_passed = sem("pool_passed")
        setup_pe, setup_dve, setup_act = sem("setup_pe"), sem("setup_dve"), sem("setup_act")
        x_in, xr_in = sem("x_in"), [sem(f"xr_in{n}") for n in range(4)]
        veps_made, rstd_made, shift_made, xn_made = sem("veps_made"), sem("rstd_made"), sem("shift_made"), sem("xn_made")
        mod_now_made = sem("mod_now_made")
        tp_full, tp_free = [sem(f"tp_full{n}") for n in range(2)], [sem(f"tp_free{n}") for n in range(2)]
        sc_full, sc_free = [sem(f"sc_full{n}") for n in range(2)], [sem(f"sc_free{n}") for n in range(2)]
        po_full, po_free = sem("po_full"), sem("po_free")
        misc_full, misc_free = sem("misc_full"), sem("misc_free")
        hsum_made = sem("hsum_made")
        masked, exp_made, pm_made = sem("masked"), sem("exp_made"), sem("pm_made")
        x1_made, x1_stored = sem("x1_made"), [sem(f"x1_stored{n}") for n in range(2)]
        veps2_made, rstd2_made, shift2_made = sem("veps2_made"), sem("rstd2_made"), sem("shift2_made")
        xn2_made, h2_scaled, h2_made = sem("xn2_made"), sem("h2_scaled"), sem("h2_made")
        routed_exp, exp_routed = sem("routed_exp"), sem("exp_routed")
        chosen_made, slots_made, scattered = sem("chosen_made"), sem("slots_made"), sem("scattered")
        rows_sent = sem("rows_sent")
        table_made, padded = sem("table_made"), sem("padded")
        hin_in = [sem(f"hin_in{n}") for n in range(UN)]
        hTp_full, hinT_made = sem("hTp_full"), sem("hinT_made")
        gu_full, act_made, fused_made = sem("gu_full"), sem("act_made"), sem("fused_made")
        fTp_full, fusedT_made, y_full, y_made = sem("fTp_full"), sem("fusedT_made"), sem("y_full"), sem("y_made")
        extra_made = sem("extra_made")
        y_out = [sem(f"y_out{n}") for n in range(UN)]
        gb_in = [sem(f"gb_in{n}") for n in range(UN)]
        out_done = sem("out_done")

        block = ctx.enter_context(nc.Block())

        wmod_sb = qv[:, 0:DC * 6 * D].rearrange("p (c n) -> p c n", c=DC)
        cond_sb = pen[0:B, 0:D]
        out_rows = out.rearrange("b s d -> (b s) d")
        x_rows = x.rearrange("b s d -> (b s) d")

        @block.sync
        def _(sp):
            sp.dma_start(cond_sb, cond[:, :]).then_inc(cond_in, 16)
            sp.dma_start(xb[:, :, :], x[0, :, :].rearrange("(t p) d -> p t d", p=P)).then_inc(x_in, 16)
            sp.dma_start(attn_sb[:, :, :], attn_w.rearrange("(c p) n -> p c n", p=P)).then_inc(attn_in, 16)
            sp.dma_start(wmod_sb, w_mod.rearrange("(c p) n -> p c n", p=P)).then_inc(wmod_in, 16)
            sp.dma_start(router_sb[:, :, :], router.rearrange("(c p) n -> p c n", p=P)).then_inc(router_in, 16)
            sp.wait_ge(setup_dve, 4)
            sp.dma_start(mod_hbm[:, :], mod_flat[:, 0:3, :].rearrange("b j d -> b (j d)")).then_inc(mod_out, 16)
            sp.dma_start(gb_hbm[:, :], mod_flat[:, 3, :]).then_inc(mod_out, 16)
            sp.wait_ge(mod_out, 32)
            sp.dma_start(mod_rows[:, :, :, :].rearrange("p b j d -> p (b j d)"),
                         mod_hbm.rearrange("b n -> (b n)").unsqueeze(0).to_broadcast([P, B * 3 * D])).then_inc(mod_in, 16)
            sp.wait_ge(consts_made, 2)
            sp.dma_start(rows_hbm[DUMMY:DUMMY + P, :], pad_row[:, :]).then_inc(pads_out, 16)
            sp.dma_start(sum_hbm[TOK:TOK + P, :], pad_row[:, 0:D]).then_inc(pads_out, 16)

            def batch(b, first, last):
                if not last:
                    for n in range(2):
                        sp.wait_ge(sc_full[n], nth(b, SC_USES, 1))
                    sp.dma_start(xb[:, :, :], x[bass.ds(b + 1, 1), :, :].rearrange("a (t p) d -> p (a t) d", p=P)
                                 ).then_inc(x_in, 16)
                for pos in range(-1, NT):
                    if pos + 1 < NT:
                        sp.wait_ge(x1_made, nth(b, NT, pos + 1))
                        tile = b * NT + ORDER[pos + 1]
                        sp.dma_start(xr[:, (pos + 1) % 4, :], x_rows[bass.ds(tile * P, P), :]
                                     ).then_inc(xr_in[(pos + 1) % 4], 16)
                    if pos >= 0:
                        sp.wait_ge(x1_made, nth(b, NT, pos + 4))
                        tile = b * NT + ORDER[pos]
                        sp.dma_start(sum_hbm[bass.ds(tile * P, P), :], x1[:, pos % 2, :]).then_inc(x1_stored[pos % 2], 16)
                if first:
                    for e in range(E):
                        for dst, src in ((gate_sb, w_gate), (up_sb, w_up), (down_sb, w_down)):
                            sp.dma_start(dst[:, e, :, :], src[e].rearrange("(c p) n -> p c n", p=P)).then_inc(expert_in, 16)

            batch(0, True, False)
            with sp.Fori(1, B - 1) as b:
                batch(b, False, False)
            batch(B - 1, False, True)

            sp.wait_ge(table_made, 2)
            for e in range(E):
                at = sp.value_load(pad_i[0:1, e:e + 1], min_val=0, max_val=E * REG)
                sp.dma_start(rows_hbm[bass.ds(at, P), :], pad_row[:, :]).then_inc(padded, 16)
            sp.wait_ge(padded, 16 * E)
            sp.wait_ge(scattered, 16 * 2 * NTT)
            sp.wait_ge(pads_out, 32)

            def load_rows(t, n):
                at = sp.value_load(tile_row_i[0:1, bass.ds(t, 1)], min_val=0, max_val=DUMMY)
                sp.dma_start(hin[:, n, :], rows_hbm[bass.ds(at, P), :]).then_inc(hin_in[n], 16)

            for t in range(UN):
                load_rows(t, t)

            def refill(t, n):
                sp.wait_ge(hTp_full, t + 1)
                sp.wait_ge(extra_made, t + 1)
                load_rows(t + UN, n)

            with sp.Fori(0, TILES // UN - 1) as i:
                for u in range(UN):
                    refill(UN * i + u, u)
            for t in range(UN * (TILES // UN - 1), TILES - UN):
                refill(t, t % UN)

            for n in range(UN):
                sp.wait_ge(y_out[n], 16 * ((TILES + UN - 1 - n) // UN))
            sp.dma_start(out_rows, sum_hbm[0:TOK, :]).then_inc(out_done, 16)
            sp.wait_ge(out_done, 16)

        @block.gpsimd
        def _(pool):
            done = [0]

            def link(ins):
                done[0] += 1
                ins.then_inc(pool_done, 1)
                pool.wait_ge(pool_done, done[0])

            def passed():
                pool.sem_inc(pool_passed, 1)

            link(pool.memset(ident[:, :], 0.0))
            pool.affine_select(out=ident[:, :], in_=ident[:, :], compare_op=ALU.not_equal, fill=1.0, base=0,
                               pattern=[[-1, P]], channel_multiplier=1).then_inc(consts_made, 1)
            link(pool.memset(minus_half[:, :], -0.5))
            pool.wait_ge(veps_made, 1)
            pool.tensor_tensor(rstd[:, :], veps[:, :], minus_half[:, :], ALU.pow).then_inc(rstd_made, 1)
            link(pool.memset(upper[:, :], 1.0))
            link(pool.affine_select(out=upper[:, :], in_=upper[:, :], compare_op=ALU.is_ge, fill=0.0, base=0,
                                    pattern=[[1, P]], channel_multiplier=-1))
            link(pool.memset(before[:, :], 1.0))
            link(pool.affine_select(out=before[:, :], in_=before[:, :], compare_op=ALU.is_ge, fill=0.0, base=-1,
                                    pattern=[[1, P]], channel_multiplier=-1))
            link(pool.memset(ones[:, :], 1.0))
            link(pool.memset(neg_col[:, :], MASK_NEG))
            link(pool.memset(pm_rows[:, :, :].rearrange("p a b -> p (a b)"), 0.0))
            link(pool.memset(seen[:, 0, :], 0.0))
            link(pool.memset(lower8[:, :, :].rearrange("p a b -> p (a b)"), 1.0))
            link(pool.affine_select(out=lower8[:, :, :], in_=lower8[:, :, :], compare_op=ALU.is_ge, fill=0.0, base=0,
                                    pattern=[[1, E], [-1, E]], channel_multiplier=0))
            link(pool.memset(pad_row[:, :], 0.0))
            for dst, pattern, n, base, per_row in (
                    (pad_row[:, D + 1:D + 2], [[0, 1]], 1, TOK, 1),
                    (region[:, :], [[REG, E]], E, 0, 0),
                    (choice_rank[:, :], [[-1, E]], E, E, 0),
                    (steps32[:, :], [[P, NTT]], NTT, 0, 0),
                    (token_of[:, :, 0], [[P, NTT]], NTT, 0, 1),
                    (token_of[:, :, 1], [[1, B], [0, NT]], NTT, 0, 0)):
                link(pool.iota(int_tmp[:, 0:n], pattern=pattern, base=base, channel_multiplier=per_row))
                link(pool.tensor_copy(dst, int_tmp[:, 0:n]))
            link(pool.iota(int_tmp[0:1, 0:TILES], pattern=[[1, TILES]], base=0, channel_multiplier=0))
            link(pool.tensor_copy(tile_no[:, :], int_tmp[0:1, 0:TILES]))
            pool.nop().then_inc(consts_made, 1)
            pool.wait_ge(mod_in, 16)

            def mod_row(b, n):
                return mod_rows[:, bass.ds(b, 1), n, :].rearrange("p a d -> p (a d)")

            def scatter(c):
                for t in range(NT):
                    pool.indirect_dma_start(
                        out=rows_hbm[:, :], out_offset=bass.IndirectOffsetOnAxis(ap=slot_i[:, c, t:t + 1], axis=0),
                        in_=h2[:, t, :], in_offset=None).then_inc(scattered, 16)

            def send_rows(b):
                pool.wait_ge(slots_made, nth(b, 1, 0))
                passed()
                for c in range(2):
                    link(pool.tensor_copy(h2[:, :, D:D + 3], extra[:, c, :, :]))
                    scatter(c)
                    pool.wait_ge(scattered, b * (16 * 2 * NT) + 16 * NT * (c + 1))
                    passed()
                pool.sem_inc(rows_sent, 1)

            def batch(b, first, last):
                pool.sem_clear(pool_done)
                done[0] = 0
                for k in range(1, NT + 1):
                    if k == 4 and not last:
                        pool.wait_ge(veps_made, nth(b + 1, 1, 0))
                        pool.tensor_tensor(rstd[:, :], veps[:, :], minus_half[:, :], ALU.pow).then_inc(rstd_made, 1)
                    if 0 <= k - 1 < NT:
                        pos = k - 1
                        if pos == 0 and not first:
                            send_rows(b - 1)
                        pool.wait_ge(veps2_made, nth(b, NT, pos))
                        pool.tensor_tensor(rstd2[:, pos % 2:pos % 2 + 1], veps2[:, pos % 2:pos % 2 + 1],
                                           minus_half[:, 0:1], ALU.pow).then_inc(rstd2_made, 1)
                        pool.wait_ge(h2_scaled, nth(b, NT, pos))
                        passed()
                        pool.tensor_tensor(h2[:, ORDER[pos], 0:D], h2[:, ORDER[pos], 0:D], mod_row(b, 1), ALU.add
                                           ).then_inc(h2_made, 1)

            batch(0, True, False)
            with pool.Fori(1, B - 1) as b:
                batch(b, False, False)
            batch(B - 1, False, True)
            pool.sem_clear(pool_done)
            done[0] = 0
            send_rows(B - 1)

            def take_extra(t, n, arrived):
                pool.wait_ge(hin_in[n], arrived)
                passed()
                pool.tensor_copy(row_weight[:, n, :], hin[:, n, D:D + 1])
                pool.tensor_copy(place_i[:, n, :], hin[:, n, D + 1:D + 3]).then_inc(extra_made, 1)

                pool.wait_ge(extra_made, t + 1)
                passed()
                pool.indirect_dma_start(
                    out=gb_rows[:, n, :], out_offset=None, in_=gb_hbm[:, :],
                    in_offset=bass.IndirectOffsetOnAxis(ap=place_i[:, n, 1:2], axis=0)).then_inc(gb_in[n], 16)

            def send_y(t, n, sent=None):
                pool.wait_ge(y_made, t + 1)
                passed()
                if sent is not None:
                    pool.wait_ge(y_out[(n - 1) % UN], sent)
                    passed()
                pool.indirect_dma_start(
                    out=sum_hbm[:, :], out_offset=bass.IndirectOffsetOnAxis(ap=place_i[:, n, 0:1], axis=0),
                    in_=y_sb[:, n, :], in_offset=None, compute_op=ALU.add).then_inc(y_out[n], 16)

            for n in range(2):
                pool.wait_ge(x1_stored[n], 16 * (NTT // 2) + 16)
            pool.wait_ge(pads_out, 32)
            for t in range(UN):
                take_extra(t, t, 16)
            send_y(0, 0)
            with pool.Fori(0, TILES // UN - 1) as i:
                for u in range(UN):
                    pool.wait_ge(y_out[u], 16 * i + 16)
                    passed()
                    take_extra(UN * i + UN + u, u, 16 * i + 32)
                    send_y(UN * i + 1 + u, (u + 1) % UN)
            for t in range(TILES // UN * UN, TILES):
                pool.wait_ge(y_out[t % UN], 16 * (t // UN))
                take_extra(t, t % UN, 16 * (t // UN + 1))
                send_y(t - UN + 1, (t + 1) % UN)
            for t in range(TILES - UN + 1, TILES):
                send_y(t, t % UN, 16 * ((t - 1) // UN + 1))

        @block.scalar
        def _(act):
            act.wait_ge(setup_pe, 1)
            act.activation(silu_c[:, :, :].rearrange("p c b -> p (c b)"), pmisc[:, 0:DC * B], ACT.Silu
                           ).then_inc(setup_act, 1)

            def normalise(b):
                act.wait_ge(shift_made, nth(b, 1, 0))
                for t in range(NT):
                    act.activation(xb[:, t, :], xb[:, t, :], ACT.Identity, bias=shift[:, t:t + 1],
                                   scale=rstd[:, t:t + 1]).then_inc(xn_made, 1)

            normalise(0)
            act.wait_ge(consts_made, 2)

            def h2T_out(b, it, pos):
                act.wait_ge(tp_full[TPU.buf(it, ("h", pos))], TPU.full(it, ("h", pos)))
                act.copy(h2T[:, pos % 2, :], tp[TPU.buf(it, ("h", pos))][:, 0:D]
                         ).then_inc(tp_free[TPU.buf(it, ("h", pos))], 1)

            def route_exps(b):
                for n, flat in enumerate((rt[0][:, :, :].rearrange("p t e -> p (t e)"), rs[2][:, :])):
                    act.wait_ge(routed_exp, nth(b, 2, n))
                    act.activation(flat, flat, ACT.Exp).then_inc(exp_routed, 1)

            def batch(b, first, last):
                act.wait_ge(mod_now_made, nth(b, 1, 0))
                for half in range(2):
                    act.wait_ge(sc_full[0], nth(b, SC_USES, half))
                    act.activation(hT[:, 0, half * HALF:(half + 1) * HALF], sc[0][:, half * HALF:(half + 1) * HALF],
                                   ACT.Identity, bias=mod_now[:, 0:1], scale=mod_now[:, DC:DC + 1]
                                   ).then_inc(sc_free[0], 1)
                if not first:
                    h2T_out(b - 1, b, TAIL[0][0])
                act.wait_ge(sc_full[0], nth(b, SC_USES, 2))
                act.copy(qT[:, 0, :], sc[0][:, :]).then_inc(sc_free[0], 1)
                if not first:
                    h2T_out(b - 1, b, TAIL[1][0])

                def v_out(i):
                    n = TPU.buf(b, ("v", i))
                    act.wait_ge(tp_full[n], TPU.full(b, ("v", i)))
                    act.copy(v_sb[:, 2 * i:2 * i + 2, :].rearrange("p t d -> p (t d)"), tp[n][:, :]
                             ).then_inc(tp_free[n], 1)

                def exponentials(pos):
                    qi = ORDER[pos]
                    w = (NT - qi) * P
                    act.wait_ge(masked, nth(b, NT, pos))
                    act.activation(prob[:, pos % 2, 0:w], prob[:, pos % 2, 0:w], ACT.Exp,
                                   bias=negmax[:, pos:pos + 1], accum_out=rowsum[:, pos:pos + 1]).then_inc(exp_made, 1)
                    if qi > 0:
                        act.activation(pm_rows[:, pos, 0:qi], negmax[:, pos:pos + 1].to_broadcast([P, qi]),
                                       ACT.Exp, bias=neg_col[:, :]).then_inc(pm_made, 1)

                if not first:
                    h2T_out(b - 1, b, TAIL[2][0])
                v_out(0)
                v_out(1)
                exponentials(0)
                v_out(2)
                v_out(3)
                if not first:
                    route_exps(b - 1)
                for k in range(NT + 1):
                    if k < NT:
                        for g, n in groups_of(k):
                            u = TPU.buf(b, ("p", k, g))
                            act.wait_ge(tp_full[u], TPU.full(b, ("p", k, g)))
                            act.copy(probT[:, k % 2, g * P:(g + n) * P], tp[u][:, 0:n * P]).then_inc(tp_free[u], 1)
                    if k + 1 < NT:
                        exponentials(k + 1)
                    if k >= 1:
                        pos = k - 1
                        act.wait_ge(shift2_made, nth(b, NT, pos))
                        act.activation(h2[:, ORDER[pos], 0:D], x1[:, pos % 2, :], ACT.Identity,
                                       bias=shift2[:, pos % 2:pos % 2 + 1], scale=rstd2[:, pos % 2:pos % 2 + 1]
                                       ).then_inc(xn2_made, 1)
                    if 0 <= k - 3 < NT - 3:
                        h2T_out(b, b, k - 3)
                    if k == 5 and not last:
                        normalise(b + 1)

            batch(0, True, False)
            with act.Fori(1, B - 1) as b:
                batch(b, False, False)
            batch(B - 1, False, True)
            for h, _ in TAIL:
                if h is not None:
                    h2T_out(B - 1, B, h)
            route_exps(B - 1)

            def silu(t, par):
                act.wait_ge(gu_full, t + 1)
                act.activation(act_sb[:, par, :], sc[0][:, par * F:(par + 1) * F], ACT.Silu).then_inc(act_made, 1)

            def fused_out(t, par):
                act.wait_ge(fTp_full, t + 1)
                act.copy(fusedT[:, par, :], tp[1][:, :]).then_inc(fusedT_made, 1)

            silu(0, 0)
            silu(1, 1)
            fused_out(0, 0)
            with act.Fori(0, LOOPS) as i:
                for u in range(UN):
                    silu(UN * i + 2 + u, u % 2)
                    fused_out(UN * i + 1 + u, (1 + u) % 2)
            silu(TILES - 1, (TILES - 1) % 2)
            fused_out(TILES - 2, (TILES - 2) % 2)
            fused_out(TILES - 1, (TILES - 1) % 2)

        @block.vector
        def _(dve):
            done = [0]

            def link(ins):
                done[0] += 1
                ins.then_inc(dve_done, 1)
                dve.wait_ge(dve_done, done[0])

            def counted(ins):
                done[0] += 1
                ins.then_inc(dve_done, 1)

            for s, n in ((tp_free[0], 1), (tp_free[1], 1), (x1_made, 4), (h2_made, 2), (x1_stored[0], 16),
                         (x1_stored[1], 16)):
                dve.nop().then_inc(s, n)

            def ln_stats(b):
                dve.wait_ge(x_in, b * 16 + 16)
                for t in range(NT):
                    counted(dve.bn_stats(stats[:, t, :], xb[:, t, :]))
                dve.wait_ge(dve_done, done[0])
                for t in range(NT):
                    counted(dve.bn_aggr(mv[:, t, :], stats[:, t, :]))
                dve.wait_ge(dve_done, done[0])
                dve.tensor_scalar(veps[:, :], mv[:, :, 1], EPS, None, ALU.add).then_inc(veps_made, 1)

            def ln_shift(b):
                dve.wait_ge(rstd_made, nth(b, 1, 0))
                dve.scalar_tensor_tensor(out=shift[:, :], in0=mv[:, :, 0], scalar=-1.0, in1=rstd[:, :],
                                         op0=ALU.mult, op1=ALU.mult).then_inc(shift_made, 1)

            ln_stats(0)
            ln_shift(0)
            dve.wait_ge(setup_pe, 2)
            wT = hT
            dve.tensor_copy(wT[:, 0, :], sc[0][:, :]).then_inc(setup_dve, 1)
            dve.wait_ge(setup_pe, 3)
            dve.tensor_scalar(qk_sb[:, :, :].rearrange("p c d -> p (c d)"), po[:, :], float(D) ** -0.5, None, ALU.mult
                              ).then_inc(setup_dve, 1)
            dve.wait_ge(setup_pe, 4)
            cols = mod_cols[:, :, :].rearrange("p j b -> p (j b)")
            link(dve.tensor_copy(cols, pmisc[:, 0:2 * DC * B]))
            n = DC * B
            dve.tensor_scalar(cols[:, n:2 * n], cols[:, n:2 * n], 1.0, None, ALU.add).then_inc(setup_dve, 1)
            dve.wait_ge(setup_dve, 3)
            dve.wait_ge(setup_pe, 5)
            link(dve.tensor_copy(mod_flat[:, :, :].rearrange("b j d -> b (j d)"), sc[1][0:B, :]))
            link(dve.tensor_scalar(mod_flat[:, 2, :], mod_flat[:, 2, :], 1.0, None, ALU.add))
            gates = mod_flat[:, 0:4:3, :]
            sign, size = (pen[0:B, n * 2 * D:(n + 1) * 2 * D].rearrange("p (j d) -> p j d", j=2) for n in range(2))
            link(dve.tensor_scalar(sign, gates, 0.0, 2.0, ALU.is_ge, ALU.mult))
            link(dve.tensor_scalar(sign, sign, 1.0, None, ALU.subtract))
            link(dve.tensor_scalar(size, gates, -1.0, None, ALU.mult))
            link(dve.tensor_tensor(size, gates, size, ALU.max))
            link(dve.tensor_scalar(size, size, 0.25, None, ALU.max))
            dve.tensor_tensor(gates, size, sign, ALU.mult).then_inc(setup_dve, 1)
            dve.wait_ge(setup_dve, 4)
            for s in (po_free, misc_free, sc_free[0], sc_free[1], rows_sent):
                dve.nop().then_inc(s, 1)
            dve.wait_ge(consts_made, 2)
            dve.wait_ge(mod_in, 16)

            def mask(b, pos):
                qi = ORDER[pos]
                w = (NT - qi) * P
                buf = sc[pos % 2]
                dve.wait_ge(sc_full[pos % 2], nth(b, SC_USES, 3 + pos // 2))
                if pos >= 2:
                    use = ("p", pos - 2, groups_of(pos - 2)[-1][0])
                    dve.wait_ge(tp_full[TPU.buf(b, use)], TPU.full(b, use))
                link(dve.tensor_tensor(buf[:, 0:P], buf[:, 0:P], upper[:, :], ALU.mult))
                link(dve.tensor_scalar(pen[:, 0:w], buf[:, 0:w], 0.0, MASK_NEG, ALU.is_equal, ALU.mult))
                dve.tensor_tensor_reduce(out=prob[:, pos % 2, 0:w], in0=buf[:, 0:w], in1=pen[:, 0:w], scale=1.0,
                                         scalar=MASK_NEG if qi > 0 else LOWEST, op0=ALU.add, op1=ALU.max,
                                         accum_out=rowmax[:, pos:pos + 1]).then_inc(sc_free[pos % 2], 1)
                dve.wait_ge(sc_free[pos % 2], b * SC_USES + (3 + pos // 2 + 2))
                dve.tensor_scalar(negmax[:, pos:pos + 1], rowmax[:, pos:pos + 1], -1.0, None, ALU.mult
                                  ).then_inc(masked, 1)

            def normaliser(b, k):
                qi = ORDER[k]
                dve.wait_ge(exp_made, nth(b, NT, k))
                if qi > 0:
                    dve.wait_ge(pm_made, nth(b, NT - 1, sum(1 for q in ORDER[:k] if q > 0)))
                    link(dve.scalar_tensor_tensor(out=rowsum[:, k:k + 1], in0=pm_rows[:, k, 0:1],
                                                  scalar=float(P * qi), in1=rowsum[:, k:k + 1],
                                                  op0=ALU.mult, op1=ALU.add))
                link(dve.reciprocal(rinv[:, k:k + 1], rowsum[:, k:k + 1]))

            def pmT_out(b, k):
                if ORDER[k] > 0:
                    dve.wait_ge(misc_full, MISCU.full(b, ("pm", k)))
                    dve.tensor_copy(pmT[:, k % 2, :], pmisc[0:NT, 0:P]).then_inc(misc_free, 1)

            def residual(b, pos):
                dve.wait_ge(po_full, nth(b, NT, pos))
                dve.wait_ge(h2_made, nth(b, NT, pos))
                dve.wait_ge(x1_stored[pos % 2], b * (8 * NT) + 16 * (pos // 2 + 1))
                dve.scalar_tensor_tensor(out=x1[:, pos % 2, :], in0=po[:, 0:D], scalar=rinv[:, pos:pos + 1],
                                         in1=mod_rows[:, bass.ds(b, 1), 0, :].rearrange("p a d -> p (a d)"),
                                         op0=ALU.mult, op1=ALU.mult).then_inc(po_free, 1)
                dve.wait_ge(po_free, b * NT + (pos + 2))
                dve.wait_ge(xr_in[pos % 4], b * 32 + 16 * (pos // 4 + 1))
                dve.tensor_tensor(x1[:, pos % 2, :], x1[:, pos % 2, :], xr[:, pos % 4, :], ALU.add).then_inc(x1_made, 1)
                dve.wait_ge(x1_made, b * NT + (pos + 5))
                link(dve.bn_stats(stats2[:, :], x1[:, pos % 2, :]))
                link(dve.bn_aggr(mv2[:, pos % 2, :], stats2[:, :]))
                dve.tensor_scalar(veps2[:, pos % 2:pos % 2 + 1], mv2[:, pos % 2, 1:2], EPS, None, ALU.add
                                  ).then_inc(veps2_made, 1)

            def shift_of(b, pos):
                dve.wait_ge(rstd2_made, nth(b, NT, pos))
                n = pos % 2
                dve.scalar_tensor_tensor(out=shift2[:, n:n + 1], in0=mv2[:, n, 0:1], scalar=-1.0, in1=rstd2[:, n:n + 1],
                                         op0=ALU.mult, op1=ALU.mult).then_inc(shift2_made, 1)

            def scale_h2(b, pos):
                dve.wait_ge(xn2_made, nth(b, NT, pos))
                dve.tensor_tensor(h2[:, ORDER[pos], 0:D], h2[:, ORDER[pos], 0:D],
                                  mod_rows[:, bass.ds(b, 1), 2, :].rearrange("p a d -> p (a d)"), ALU.mult
                                  ).then_inc(h2_scaled, 1)

            def logits_out(it, pos):
                dve.wait_ge(misc_full, MISCU.full(it, ("lg", pos)))
                dve.tensor_copy(lg[:, ORDER[pos], :], pmisc[:, 0:E]).then_inc(misc_free, 1)

            def batch(b, first, last):
                done[0] = 0
                dve.sem_clear(dve_done)
                dve.tensor_copy(mod_now[:, :], mod_cols[:, :, bass.ds(b, 1)].rearrange("p j a -> p (j a)")
                                ).then_inc(mod_now_made, 1)
                dve.wait_ge(mod_now_made, nth(b, 1, 0))
                for half in range(2):
                    dve.wait_ge(sc_full[1], nth(b, SC_USES, half))
                    dve.tensor_scalar(hT[:, 1, half * HALF:(half + 1) * HALF], sc[1][:, half * HALF:(half + 1) * HALF],
                                      mod_now[:, DC + 1:DC + 2], mod_now[:, 1:2], ALU.mult, ALU.add
                                      ).then_inc(sc_free[1], 1)
                if not first:
                    logits_out(b, TAIL[0][1])
                dve.wait_ge(sc_full[1], nth(b, SC_USES, 2))
                dve.tensor_copy(qT[:, 1, :], sc[1][:, :]).then_inc(sc_free[1], 1)
                if not first:
                    logits_out(b, TAIL[1][1])
                mask(b, 0)
                for c in range(DC):
                    dve.wait_ge(sc_free[c], b * SC_USES + 3)
                dve.tensor_reduce(hsum[:, :, :].rearrange("p c t -> p (c t)"),
                                  hT[:, :, :].rearrange("p c (t s) -> p (c t) s", s=P), AX.X, ALU.add
                                  ).then_inc(hsum_made, 1)
                if not first:
                    logits_out(b, TAIL[2][1])
                    logits_out(b, TAIL[3][1])
                mask(b, 1)
                if not first:
                    route(b - 1, b)
                dve.wait_ge(misc_full, MISCU.full(b, "vsum"))
                dve.tensor_copy(vsum[:, :], pmisc[0:NT, 0:D]).then_inc(misc_free, 1)
                dve.wait_ge(misc_free, MISCU.read(b, "vsum"))
                for k in range(NT + 1):
                    if k < NT:
                        if 1 <= k and k + 1 < NT:
                            mask(b, k + 1)
                        normaliser(b, k)
                        pmT_out(b, k)
                    if k >= 1:
                        residual(b, k - 1)
                        if k - 2 >= 0:
                            scale_h2(b, k - 2)
                        shift_of(b, k - 1)
                    if 0 <= k - 4 < NT - 4:
                        logits_out(b, k - 4)
                    if k == 2 and not last:
                        ln_stats(b + 1)
                    if k == 4 and not last:
                        ln_shift(b + 1)
                scale_h2(b, NT - 1)
                dve.wait_ge(h2_scaled, nth(b, NT, NT - 1))

            def route(b, it):
                p3, t3, q3 = (r[:, :, :] for r in rt)
                s0, s1, s2, s3 = (r[:, :] for r in rs)

                def wide(s):
                    return s.unsqueeze(2).to_broadcast([P, NT, E])

                dve.wait_ge(misc_free, MISCU.read(it, ("lg", NT - 1)))
                link(dve.tensor_reduce(s0, lg[:, :, :], AX.X, ALU.max))
                dve.tensor_tensor(p3, lg[:, :, :], wide(s0), ALU.subtract).then_inc(routed_exp, 1)
                dve.wait_ge(exp_routed, nth(b, 2, 0))
                link(dve.tensor_reduce(s0, p3, AX.X, ALU.add))
                link(dve.reciprocal(s1, s0))
                link(dve.tensor_tensor(p3, p3, wide(s1), ALU.mult))
                rank3 = choice_rank[:, :].unsqueeze(1).to_broadcast([P, NT, E])
                region3 = region[:, :].unsqueeze(1).to_broadcast([P, NT, E])
                for c, top in ((0, s0), (1, s1)):
                    one_hot = pick[:, c, :, :]
                    link(dve.tensor_reduce(top, p3, AX.X, ALU.max))
                    link(dve.tensor_tensor(t3, p3, wide(top), ALU.is_equal))
                    link(dve.tensor_tensor(t3, t3, rank3, ALU.mult))
                    link(dve.tensor_reduce(s3, t3, AX.X, ALU.max))
                    link(dve.tensor_tensor(one_hot, t3, wide(s3), ALU.is_equal))
                    if c == 0:
                        link(dve.scalar_tensor_tensor(out=p3, in0=one_hot, scalar=-2.0, in1=p3, op0=ALU.mult, op1=ALU.add))
                link(dve.tensor_tensor(chosen[:, :, :], pick[:, 0, :, :], pick[:, 1, :, :], ALU.add))
                for t in range(NT):
                    ins = dve.tensor_tensor(seen[:, t + 1, :], seen[:, t, :], chosen[:, t, :], ALU.add)
                    if t < NT - 1:
                        link(ins)
                ins.then_inc(chosen_made, 1)
                dve.tensor_tensor(s2, s1, s0, ALU.subtract).then_inc(routed_exp, 1)
                dve.wait_ge(rows_sent, nth(b, 1, 0))
                for c in range(2):
                    counted(dve.tensor_copy(extra[:, c, :, 1:3], token_of[:, bass.ds(b * NT, NT), :]))
                dve.wait_ge(exp_routed, nth(b, 2, 1))
                link(dve.tensor_scalar(s3, s2, 1.0, None, ALU.add))
                link(dve.reciprocal(s0, s3))
                counted(dve.tensor_copy(extra[:, 0, :, 0], s0))
                counted(dve.tensor_tensor(extra[:, 1, :, 0], s2, s0, ALU.mult))
                dve.wait_ge(misc_full, MISCU.full(it, "rank"))
                dve.tensor_tensor(t3, pmisc[:, 0:NT * E].rearrange("p (t e) -> p t e", e=E), region3, ALU.add
                                  ).then_inc(misc_free, 1)
                dve.wait_ge(misc_free, MISCU.read(it, "rank"))
                for c in range(2):
                    link(dve.tensor_tensor(q3, t3, pick[:, c, :, :], ALU.mult))
                    link(dve.tensor_reduce(slot[:, :], q3, AX.X, ALU.add))
                    ins = dve.tensor_copy(slot_i[:, c, :], slot[:, :])
                    if c == 0:
                        link(ins)
                ins.then_inc(slots_made, 1)
                link(dve.tensor_copy(seen[:, 0, :], seen[:, NT, :]))

            batch(0, True, False)
            with dve.Fori(1, B - 1) as b:
                batch(b, False, False)
            batch(B - 1, False, True)
            dve.sem_clear(dve_done)
            done[0] = 0
            for _, n in TAIL:
                logits_out(B, n)
            route(B - 1, B)

            dve.wait_ge(misc_full, MISCU.full(B, "rank") + 1)
            link(dve.tensor_copy(count[:, :], pmisc[:, 0:E]))
            g3 = grid[:, 0:E * NTT].rearrange("p (e m) -> p e m", e=E)
            link(dve.tensor_tensor(g3, count[:, :].unsqueeze(2).to_broadcast([P, E, NTT]),
                                   steps32[:, :].unsqueeze(1).to_broadcast([P, E, NTT]), ALU.is_gt))
            link(dve.tensor_reduce(tiles_of[:, :], g3, AX.X, ALU.add))
            g8 = grid[:, 0:E * E].rearrange("p (a b) -> p a b", a=E)
            link(dve.tensor_tensor(g8, lower8[:, :, :], tiles_of[:, :].unsqueeze(1).to_broadcast([P, E, E]), ALU.mult))
            link(dve.tensor_reduce(end_of[:, :], g8, AX.X, ALU.add))
            ge = grid[0:1, :].rearrange("p (t e) -> p t e", e=E)
            gs = grid2[0:1, :].rearrange("p (t e) -> p t e", e=E)
            wide_t = tile_no[:, :].unsqueeze(2).to_broadcast([1, TILES, E])
            link(dve.tensor_tensor(ge, wide_t, end_of[0:1, :].unsqueeze(1).to_broadcast([1, TILES, E]), ALU.is_ge))
            link(dve.tensor_tensor(gs, ge, tiles_of[0:1, :].unsqueeze(1).to_broadcast([1, TILES, E]), ALU.mult))
            link(dve.tensor_reduce(tile_exp[:, :], ge, AX.X, ALU.add))
            link(dve.tensor_reduce(tile_row[:, :], gs, AX.X, ALU.add))
            link(dve.tensor_tensor(tile_row[:, :], tile_no[:, :], tile_row[:, :], ALU.subtract))
            link(dve.tensor_scalar(tile_row[:, :], tile_row[:, :], float(P), None, ALU.mult))
            link(dve.scalar_tensor_tensor(out=tile_row[:, :], in0=tile_exp[:, :], scalar=float(REG), in1=tile_row[:, :],
                                          op0=ALU.mult, op1=ALU.add))
            link(dve.tensor_scalar(tile_row[:, :], tile_row[:, :], float(DUMMY), None, ALU.min))
            link(dve.tensor_copy(tile_row_i[:, :], tile_row[:, :]))
            link(dve.tensor_scalar(tile_exp[:, :], tile_exp[:, :], float(E - 1), None, ALU.min))
            dve.tensor_copy(tile_exp_i[:, :], tile_exp[:, :]).then_inc(table_made, 1)
            link(dve.tensor_tensor(pad_at[:, :], count[0:1, :], region[0:1, :], ALU.add))
            dve.tensor_copy(pad_i[:, :], pad_at[:, :]).then_inc(table_made, 1)

            def rows_out(t, par):
                dve.wait_ge(hTp_full, t + 1)
                dve.tensor_copy(hinT[:, par, :], tp[0][:, 0:D]).then_inc(hinT_made, 1)

            def product(t, par):
                dve.wait_ge(act_made, t + 1)
                dve.tensor_tensor(fused[:, par, :], act_sb[:, par, :], sc[1][:, par * F:(par + 1) * F], ALU.mult
                                  ).then_inc(fused_made, 1)

            def y_to_sbuf(t, n, sent, arrived):
                dve.wait_ge(extra_made, t + 1)
                dve.wait_ge(y_full, t + 1)
                if sent is not None:
                    dve.wait_ge(y_out[n], sent)
                dve.wait_ge(gb_in[n], arrived)
                dve.scalar_tensor_tensor(out=y_sb[:, n, :], in0=(po if n % 2 == 0 else pmisc)[:, 0:D],
                                         scalar=row_weight[:, n, :], in1=gb_rows[:, n, :],
                                         op0=ALU.mult, op1=ALU.mult).then_inc(y_made, 1)

            rows_out(0, 0)
            rows_out(1, 1)
            product(0, 0)
            product(1, 1)
            rows_out(2, 0)

            def step(t, u, sent, arrived):
                product(t + 1, (u + 1) % 2)
                rows_out(t + 2, u % 2)
                y_to_sbuf(t - 1, (u - 1) % UN, sent, arrived)

            for t in range(1, UN + 1):
                step(t, t, None, 16)
            with dve.Fori(1, LOOPS) as i:
                for u in range(UN):
                    step(UN * i + 1 + u, u + 1, 16 * i, 16 * i + 16)
            product(TILES - 1, (TILES - 1) % 2)
            for t in range(TILES - 3, TILES):
                y_to_sbuf(t, t % UN, 16 * (t // UN), 16 * (t // UN + 1))

        @block.tensor
        def _(pe):
            pe.wait_ge(consts_made, 1)
            pe.wait_ge(cond_in, 16)
            for c in range(DC):
                mm = pe.transpose(pmisc[:, c * B:(c + 1) * B], cond_sb[:, c * P:(c + 1) * P], ident[0:B, 0:B])
            mm.then_inc(setup_pe, 1)
            pe.wait_ge(attn_in, 16)
            for j in range(2):
                for f in range(DC):
                    for c in range(DC):
                        o = (j * DC + f) * D + c * P
                        mm = pe.transpose(sc[0][:, o:o + P], attn_sb[:, c, j * D + f * P:j * D + (f + 1) * P], ident[:, :])
            mm.then_inc(setup_pe, 1)
            pe.wait_ge(setup_dve, 1)
            for i in range(DC):
                for f in range(DC):
                    mm = pe.matmul(po[:, i * D:(i + 1) * D], hT[:, 0, f * D + i * P:f * D + (i + 1) * P],
                                   hT[:, 0, (DC + f) * D:(DC + f + 1) * D], start=(f == 0), stop=(f == DC - 1))
            mm.then_inc(setup_pe, 1)
            pe.wait_ge(setup_act, 1)
            pe.wait_ge(wmod_in, 16)
            for j in range(2 * DC):
                for c in range(DC):
                    mm = pe.matmul(pmisc[:, j * B:(j + 1) * B], wmod_sb[:, c, j * P:(j + 1) * P], silu_c[:, c, :],
                                   start=(c == 0), stop=(c == DC - 1))
            mm.then_inc(setup_pe, 1)
            for half in range(2):
                for c in range(DC):
                    o = 2 * D + half * 512
                    mm = pe.matmul(sc[1][0:B, half * 512:(half + 1) * 512], silu_c[:, c, :],
                                   wmod_sb[:, c, o:o + 512], start=(c == 0), stop=(c == DC - 1))
            mm.then_inc(setup_pe, 1)
            pe.wait_ge(router_in, 16)

            def h2_transposed(b, it, pos):
                u = ("h", pos)
                pe.wait_ge(h2_made, nth(b, NT, pos + 2))
                pe.wait_ge(tp_free[TPU.buf(it, u)], TPU.full(it, u))
                for c in range(DC):
                    mm = pe.transpose(tp[TPU.buf(it, u)][:, c * P:(c + 1) * P], h2[:, ORDER[pos], c * P:(c + 1) * P],
                                      ident[:, :])
                mm.then_inc(tp_full[TPU.buf(it, u)], 1)

            def logits(it_h, it, pos):
                pe.wait_ge(tp_free[TPU.buf(it_h, ("h", pos))], TPU.read(it_h, ("h", pos)))
                pe.wait_ge(misc_free, MISCU.full(it, ("lg", pos)))
                for c in range(DC):
                    mm = pe.matmul(pmisc[:, 0:E], h2T[:, pos % 2, c * P:(c + 1) * P], router_sb[:, c, :],
                                   start=(c == 0), stop=(c == DC - 1))
                mm.then_inc(misc_full, 1)

            def tail(it, n):
                h, l = TAIL[n]
                if h is not None:
                    h2_transposed(it - 1, it, h)
                logits(it - 1 if n == 0 else it, it, l)

            def ranks(b, it):
                pe.wait_ge(chosen_made, nth(b, 1, 0))
                pe.wait_ge(misc_free, MISCU.full(it, "rank"))
                pe.matmul(pmisc[:, 0:NT * E], before[:, :], chosen[:, :, :].rearrange("p t e -> p (t e)"),
                          start=True, stop=False)
                pe.matmul(pmisc[:, 0:NT * E], ones[:, :], seen[:, 0:NT, :].rearrange("p t e -> p (t e)"),
                          start=False, stop=True).then_inc(misc_full, 1)

            def batch(b, first, last):
                for c in range(DC):
                    pe.wait_ge(sc_free[c], nth(b, SC_USES, 0))
                for half in range(2):
                    for t in range(half * NT // 2, (half + 1) * NT // 2):
                        pe.wait_ge(xn_made, nth(b, NT, t))
                        for c in range(DC):
                            mm = pe.transpose(sc[c][:, t * P:(t + 1) * P], xb[:, t, c * P:(c + 1) * P], ident[:, :])
                            if t == (half + 1) * NT // 2 - 1:
                                mm.then_inc(sc_full[c], 1)
                if not first:
                    tail(b, 0)
                for f in range(DC):
                    for c in range(DC):
                        pe.wait_ge(sc_free[c], b * SC_USES + 3)
                    for half in range(2):
                        for c in range(DC):
                            mm = pe.matmul(sc[f][:, half * HALF:(half + 1) * HALF], qk_sb[:, c, f * P:(f + 1) * P],
                                           hT[:, c, half * HALF:(half + 1) * HALF], start=(c == 0), stop=(c == DC - 1))
                    mm.then_inc(sc_full[f], 1)
                if not first:
                    tail(b, 1)

                def scores(pos):
                    qi = ORDER[pos]
                    w = (NT - qi) * P
                    pe.wait_ge(sc_free[pos % 2], nth(b, SC_USES, 3 + pos // 2))
                    for o in range(0, w, 512):
                        n = min(512, w - o)
                        for c in range(DC):
                            mm = pe.matmul(sc[pos % 2][:, o:o + n], qT[:, c, qi * P:(qi + 1) * P],
                                           hT[:, c, qi * P + o:qi * P + o + n], start=(c == 0), stop=(c == DC - 1))
                    mm.then_inc(sc_full[pos % 2], 1)

                def values(pos):
                    qi = ORDER[pos]
                    pe.wait_ge(po_free, nth(b, NT, pos))
                    for g, n in groups_of(pos):
                        u = ("p", pos, g)
                        pe.wait_ge(tp_free[TPU.buf(b, u)], TPU.read(b, u))
                        for i in range(n):
                            j = g + i
                            mm = pe.matmul(po[:, 0:D], probT[:, pos % 2, j * P:(j + 1) * P], v_sb[:, qi + j, :],
                                           start=(j == 0), stop=(j == NT - 1 - qi and qi == 0))
                    if qi > 0:
                        pe.wait_ge(misc_free, MISCU.read(b, ("pm", pos)))
                        mm = pe.matmul(po[:, 0:D], pmT[:, pos % 2, :], vsum[:, :], start=False, stop=True)
                    mm.then_inc(po_full, 1)

                for f in range(DC):
                    pe.wait_ge(sc_free[f], b * SC_USES + 4)
                scores(0)
                if not first:
                    tail(b, 2)
                for i in range(NT // 2):
                    u = ("v", i)
                    pe.wait_ge(tp_free[TPU.buf(b, u)], TPU.full(b, u))
                    for t in (2 * i, 2 * i + 1):
                        for c in range(DC):
                            mm = pe.matmul(tp[TPU.buf(b, u)][:, (t % 2) * D:(t % 2 + 1) * D], hT[:, c, t * P:(t + 1) * P],
                                           attn_sb[:, c, 2 * D:3 * D], start=(c == 0), stop=(c == DC - 1))
                    mm.then_inc(tp_full[TPU.buf(b, u)], 1)
                if not first:
                    tail(b, 3)
                scores(1)
                if not first:
                    ranks(b - 1, b)
                pe.wait_ge(hsum_made, nth(b, 1, 0))
                pe.wait_ge(misc_free, MISCU.full(b, "vsum"))
                for c in range(DC):
                    mm = pe.matmul(pmisc[0:NT, 0:D], hsum[:, c, :], attn_sb[:, c, 2 * D:3 * D],
                                   start=(c == 0), stop=(c == DC - 1))
                mm.then_inc(misc_full, 1)
                for i in range(NT // 2):
                    pe.wait_ge(tp_free[TPU.buf(b, ("v", i))], TPU.read(b, ("v", i)))
                for k in range(NT + 1):
                    if 1 <= k and k + 1 < NT:
                        scores(k + 1)
                    if k >= 1:
                        values(k - 1)
                    if k < NT:
                        qi = ORDER[k]
                        pe.wait_ge(exp_made, nth(b, NT, k))
                        for g, n in groups_of(k):
                            u = ("p", k, g)
                            pe.wait_ge(tp_free[TPU.buf(b, u)], TPU.full(b, u))
                            for i in range(n):
                                mm = pe.transpose(tp[TPU.buf(b, u)][:, i * P:(i + 1) * P],
                                                  prob[:, k % 2, (g + i) * P:(g + i + 1) * P], ident[:, :])
                            mm.then_inc(tp_full[TPU.buf(b, u)], 1)
                        if qi > 0:
                            pe.wait_ge(pm_made, nth(b, NT - 1, sum(1 for q in ORDER[:k] if q > 0)))
                            pe.wait_ge(misc_free, MISCU.full(b, ("pm", k)))
                            pe.transpose(pmisc[0:NT, 0:P], pm_rows[:, k, :], ident[:, :]).then_inc(misc_full, 1)
                        if k >= 3:
                            h2_transposed(b, b, k - 3)
                        if k >= 4:
                            logits(b, b, k - 4)

            batch(0, True, False)
            with pe.Fori(1, B - 1) as b:
                batch(b, False, False)
            batch(B - 1, False, True)
            for n in range(len(TAIL)):
                tail(B, n)
            ranks(B - 1, B)
            pe.wait_ge(misc_free, MISCU.read(B, "rank"))
            pe.matmul(pmisc[:, 0:E], ones[:, :], seen[:, NT, :], start=True, stop=True).then_inc(misc_full, 1)

            pe.wait_ge(table_made, 2)
            pe.wait_ge(expert_in, 16 * 3 * E)

            def experts_of(t, n):
                return nc.values_load_multi_w_load_instructions(
                    tile_exp_i[0:1, bass.ds(t, n)], engines=[mybir.EngineType.PE], min_val=0, max_val=E - 1)[1]

            def rows_t(t, n, arrived, first=False):
                pe.wait_ge(hin_in[n], arrived)
                if not first:
                    pe.wait_ge(hinT_made, t)
                for c in range(DC):
                    mm = pe.transpose(tp[0][:, c * P:(c + 1) * P], hin[:, n, c * P:(c + 1) * P], ident[:, :])
                mm.then_inc(hTp_full, 1)

            def gate_up(t, par, e, early=False):
                pe.wait_ge(hinT_made, t + 1)
                if not early:
                    pe.wait_ge(fused_made, t - 1)
                for w, buf in ((gate_sb, sc[0]), (up_sb, sc[1])):
                    for c in range(DC):
                        mm = pe.matmul(buf[:, par * F:(par + 1) * F], hinT[:, par, c * P:(c + 1) * P],
                                       w[:, bass.ds(e, 1), c, :].rearrange("p a f -> p (a f)"),
                                       start=(c == 0), stop=(c == DC - 1))
                mm.then_inc(gu_full, 1)

            def fused_t(t, par, first=False):
                pe.wait_ge(fused_made, t + 1)
                if not first:
                    pe.wait_ge(fusedT_made, t)
                for f in range(FC):
                    mm = pe.transpose(tp[1][:, f * P:(f + 1) * P], fused[:, par, f * P:(f + 1) * P], ident[:, :])
                mm.then_inc(fTp_full, 1)

            def down(t, par, e, early=False):
                pe.wait_ge(fusedT_made, t + 1)
                if not early:
                    pe.wait_ge(y_made, t - 1)
                for f in range(FC):
                    mm = pe.matmul((po if par == 0 else pmisc)[:, 0:D], fusedT[:, par, f * P:(f + 1) * P],
                                   down_sb[:, bass.ds(e, 1), f, :].rearrange("p a d -> p (a d)"),
                                   start=(f == 0), stop=(f == FC - 1))
                mm.then_inc(y_full, 1)

            e = experts_of(0, 3)
            rows_t(0, 0, 16, first=True)
            rows_t(1, 1, 16)
            gate_up(0, 0, e[0], early=True)
            gate_up(1, 1, e[1], early=True)
            fused_t(0, 0, first=True)
            rows_t(2, 2, 16)

            def step(t, u, gate_e, down_e, arrived, early=False):
                gate_up(t + 1, (u + 1) % 2, gate_e)
                fused_t(t, u % 2)
                rows_t(t + 2, (u + 2) % UN, arrived)
                down(t - 1, (u + 1) % 2, down_e, early=early)

            experts = experts_of(0, UN + 2)
            for t in range(1, UN + 1):
                step(t, t % UN, experts[t + 1], experts[t - 1], 16 * ((t + 2) // UN + 1), early=t < 3)
            with pe.Fori(1, LOOPS) as i:
                experts = experts_of(UN * i, UN + 2)
                for u in range(1, UN + 1):
                    step(UN * i + u, u % UN, experts[u + 1], experts[u - 1], 16 * i + 16 * ((u + 2) // UN + 1))
            e = experts_of(TILES - 3, 3)
            gate_up(TILES - 1, (TILES - 1) % 2, e[2])
            fused_t(TILES - 2, (TILES - 2) % 2)
            down(TILES - 3, (TILES - 3) % 2, e[0])
            fused_t(TILES - 1, (TILES - 1) % 2)
            down(TILES - 2, (TILES - 2) % 2, e[1])
            down(TILES - 1, (TILES - 1) % 2, e[2])


_INS = ['L0_attn_x', 'L0_attn_W', 'L0_ffn_router_kernel_DE', 'L0_ffn_kernel_gating_EDF', 'L0_ffn_kernel_up_EDF',
        'L0_ffn_kernel_down_EFD', 'L0_c', 'L0_wmod']
_OUTS = [((B, S, D), 'float32')]


def kernel(**inputs):
    import numpy as _np
    import concourse.bacc as _bacc
    from concourse import mybir as _mybir
    from concourse.bass_utils import run_bass_kernel_spmd as _run

    nc = _bacc.Bacc("TRN2", target_bir_lowering=False, num_devices=1)
    arrays, args = {}, []
    for name in _INS:
        a = _np.ascontiguousarray(inputs[name])
        arrays[f"in_{name}_dram"] = a
        args.append(nc.dram_tensor(f"in_{name}_dram", a.shape, _mybir.dt.from_np(a.dtype), kind="ExternalInput").ap())
    for i, (shape, dtype) in enumerate(_OUTS):
        dt = _mybir.dt.from_np(_np.dtype(dtype))
        args.append(nc.dram_tensor(f"out_{i}_dram", shape, dt, kind="ExternalOutput").ap())
    build(nc, *args)
    r = _run(nc, [arrays], core_ids=[0])
    got = tuple(r.results[0][f"out_{i}_dram"] for i in range(len(_OUTS)))
    return got[0]
```

```python
from contextlib import ExitStack

import concourse.bass as bass
from concourse import mybir

fp32 = mybir.dt.float32
bf16 = mybir.dt.bfloat16
i32 = mybir.dt.int32
f32r = mybir.dt.float32r
ALU = mybir.AluOpType
ACT = mybir.ActivationFunctionType
AX = mybir.AxisListType

P = 128
B, S, D = 4, 1024, 256
E, F = 8, 512
DC, FC = D // P, F // P
NT = S // P
HALF = S // 2
TOK = B * S
NTT = TOK // P
MASK_NEG = -9000000000000000.0
LOWEST = -3.4028234663852886e38
EPS = 1e-5
REG = TOK + P
DUMMY = E * REG
TILES = 2 * TOK // P + E - 1
FIRST = -(-(2 * (B - 1) * S - E * (P - 1)) // P)
ROW = D + 3
UN = 4
LOOPS = (TILES - 3) // UN
assert 1 + LOOPS * UN == TILES - 2

ORDER = [0, 7, 1, 6, 2, 5, 3, 4]
assert sorted(ORDER) == list(range(NT))
POOL_LOW = [0, 1, 9, 12, 14]
GROUP = 4
OWN_H = NT - 4
OWN_LG = NT - 5

def groups_of(pos):
    n = NT - ORDER[pos]
    return [(g, min(GROUP, n - g)) for g in range(0, n, GROUP)]


class Uses:

    def __init__(self, first, later, end, buffers):
        self.first, self.later, self.end, self.n = first, later, end, buffers
        assert len(later) % buffers == 0

    def at(self, it, use):
        if isinstance(it, int) and it == 0:
            k, rounds = self.first.index(use), 0
        elif isinstance(it, int) and it == B:
            k, rounds = len(self.first) + (B - 1) * len(self.later) + self.end.index(use), 0
        else:
            k, rounds = len(self.first) + self.later.index(use), (it - 1) * (len(self.later) // self.n)
        return k % self.n, k // self.n, rounds

    def buf(self, it, use):
        return self.at(it, use)[0]

    def full(self, it, use):
        _, k, rounds = self.at(it, use)
        return rounds + (k + 1)

    def read(self, it, use):
        _, k, rounds = self.at(it, use)
        return rounds + (k + 2)


def main_uses():
    tp, misc = [], []
    for k in range(NT):
        if k >= NT - OWN_LG:
            misc.append(("lg", k - (NT - OWN_LG)))
        if k == 4:
            misc.append("rank")
        tp += [("p", k, g) for g, _ in groups_of(k)]
        if ORDER[k] > 0:
            misc.append(("pm", k))
        if k >= NT - OWN_H:
            tp.append(("h", k - (NT - OWN_H)))
    return tp, misc


TP_MAIN, MISC_MAIN = main_uses()
TPU = Uses([("v", 0), ("v", 1), ("v", 2), ("v", 3)] + TP_MAIN,
           [("h", 4), ("h", 5), ("v", 0), ("v", 1), ("h", 6), ("v", 2), ("v", 3), ("h", 7)] + TP_MAIN,
           [("h", n) for n in range(4, 8)], 2)
MISCU = Uses(["vsum"] + [u for u in MISC_MAIN if u != "rank"],
             [("lg", 3), ("lg", 4), ("lg", 5), ("lg", 6), "vsum", ("lg", 7)] + MISC_MAIN,
             [("lg", n) for n in range(3, 8)] + ["rank"], 1)
SC_USES = 3 + NT // 2
SC_FREED = 3


def nth(batch, per_batch, k):
    return batch * per_batch + (k + 1)


def build(nc, x, attn_w, router, w_gate, w_up, w_down, cond, w_mod, out):
    ctx = ExitStack()
    with ctx:
        attention = ExitStack()

        def sb(name, shape, dt=fp32, stack=ctx):
            return stack.enter_context(nc.sbuf_tensor(name, shape, dt))

        def pb(name, shape):
            return ctx.enter_context(nc.psum_tensor(name, shape, fp32))

        def sem(name):
            return ctx.enter_context(nc.semaphore(name))

        rows_hbm = nc.dram_tensor("rows_hbm", [E * REG + P, ROW], fp32, kind="Internal").ap()
        sum_hbm = nc.dram_tensor("sum_hbm", [TOK + P, D], fp32, kind="Internal").ap()
        mod_hbm = nc.dram_tensor("mod_hbm", [B, 3 * D], fp32, kind="Internal").ap()
        gb_hbm = nc.dram_tensor("gb_hbm", [B, D], fp32, kind="Internal").ap()

        down_sb = sb("down_sb", [P, E, FC, D])

        ident = sb("ident", [P, P])
        before = sb("before", [P, P], bf16)
        ones = sb("ones", [P, P], bf16)
        neg_col = sb("neg_col", [P, 1])
        pad_row = sb("pad_row", [P, ROW])
        minus_half = sb("minus_half", [P, NT])
        region = sb("region", [P, E])
        choice_rank = sb("choice_rank", [P, E])
        int_tmp = sb("int_tmp", [P, P], i32)
        token_of = sb("token_of", [P, NTT, 2])

        router_sb = sb("router_sb", [P, DC, E])
        mod_cols = sb("mod_cols", [P, 2 * DC, B])
        mod_now = sb("mod_now", [P, 2 * DC])
        silu_c = sb("silu_c", [P, DC, B])
        hsum = sb("hsum", [P, DC, NT])
        stats = sb("stats", [P, NT, 6])
        mv = sb("mv", [P, NT, 2])
        veps = sb("veps", [P, NT])
        rstd = sb("rstd", [P, NT])
        shift = sb("shift", [P, NT])
        stats2 = sb("stats2", [P, 6])
        mv2 = sb("mv2", [P, 2, 2])
        veps2 = sb("veps2", [P, 2])
        rstd2 = sb("rstd2", [P, 2])
        shift2 = sb("shift2", [P, 2])
        negmax = sb("negmax", [P, NT])
        rowsum = sb("rowsum", [P, NT])
        rinv = sb("rinv", [P, NT])

        lg = sb("lg", [P, NT, E])
        rt = [sb(f"rt{n}", [P, NT, E]) for n in range(3)]
        rs = [sb(f"rs{n}", [P, NT]) for n in range(4)]
        rank_sb = sb("rank_sb", [P, NT + 1, E])
        pick = sb("pick", [P, 2, NT, E])
        slot = sb("slot", [P, NT])
        extra = sb("extra", [P, 2, NT, 3])
        slot_i = sb("slot_i", [P, 2, NT], i32)
        chosen = sb("chosen", [P, NT, E], bf16)
        seen = sb("seen", [P, E], bf16)
        added = sb("added", [P, E])

        row_weight = sb("row_weight", [P, UN, 1])
        place_i = sb("place_i", [P, UN, 2], i32)

        full_count = sb("full_count", [P, E])
        tiles_of = sb("tiles_of", [P, E])
        full_end = sb("full_end", [P, E + 1])
        full_of = sb("full_of", [P, E + 1])
        rest_end = sb("rest_end", [P, E])
        rest_grid = sb("rest_grid", [P, 2, E * max(NTT, TILES - FIRST)])
        jump = sb("jump", [P, E])
        pad_at = sb("pad_at", [1, E])
        steps32 = sb("steps32", [P, NTT])
        lower8 = sb("lower8", [P, E, E])
        tile_no = sb("tile_no", [1, TILES])
        tile_exp = sb("tile_exp", [1, TILES])
        tile_row = sb("tile_row", [1, TILES])
        tile_exp_i = sb("tile_exp_i", [1, TILES], i32)
        tile_row_i = sb("tile_row_i", [1, TILES], i32)
        pad_i = sb("pad_i", [1, E], i32)

        HIGH = E * 2 * DC * F
        raw = sb("raw", [P, E, 2, DC * F], stack=attention)
        sizes = [DC * 3 * D, DC * D, DC * D, NT * D, DC * S, DC * S + NT * D, S, 2 * S, 2 * S, B * 3 * D]
        assert HIGH <= sum(sizes) - 3 * D
        work = sb("work", [P, sum(sizes)], stack=attention)
        parts = [work[:, sum(sizes[:n]):sum(sizes[:n + 1])] for n in range(len(sizes))]
        attn_sb = parts[0].rearrange("p (c n) -> p c n", c=DC)
        qk_sb = parts[1].rearrange("p (c d) -> p c d", c=DC)
        wv_sb = parts[2].rearrange("p (c d) -> p c d", c=DC)
        xb = parts[3].rearrange("p (t d) -> p t d", t=NT)
        hT = parts[4].rearrange("p (c s) -> p c s", c=DC)
        qv, pen = parts[5], parts[6]
        prob = parts[7].rearrange("p (r s) -> p r s", r=2)
        probT = parts[8].rearrange("p (r s) -> p r s", r=2)
        mod_rows = parts[9].rearrange("p (b j d) -> p b j d", b=B, j=3)
        xr = sb("xr", [P, 4, D], stack=attention)
        x1_h2T = sb("x1_h2T", [P, 4, D], stack=attention)
        x1, h2T = x1_h2T[:, 0:2, :], x1_h2T[:, 2:4, :]
        h2 = sb("h2", [P, NT, D], stack=attention)
        upper = sb("upper", [P, P], stack=attention)
        vsum = sb("vsum", [NT, D], stack=attention)
        pm_rows = sb("pm_rows", [P, NT, NT], stack=attention)
        pmT = sb("pmT", [NT, 2, P], stack=attention)
        h2_rows = sb("h2_rows", [P, NT, ROW], stack=attention)
        qT = qv[:, 0:DC * S].rearrange("p (c s) -> p c s", c=DC)
        v_sb = qv[:, DC * S:].rearrange("p (t d) -> p t d", t=NT)
        mod_flat = probT[0:B, 0, :].rearrange("b (j d) -> b j d", j=4)

        attention.close()
        low = sb("low", [P, E, 2, DC * F], f32r)
        high = sb("high", [P, E, 2, DC * F], f32r)
        fused = sb("fused", [P, 2, F])
        hin = sb("hin", [P, UN, ROW])
        hinT = sb("hinT", [P, 2, 2, D], f32r)
        fusedT = sb("fusedT", [P, 2, F])
        act_sb = sb("act_sb", [P, 2, F])
        y_sb = sb("y_sb", [P, UN, D])
        gb_rows = sb("gb_rows", [P, UN, D])
        grids = [fused, rest_grid]
        assert E * max(FIRST, NTT) <= F
        tp = [pb(f"tp{n}", [P, 512]) for n in range(2)]
        sc = [pb(f"sc{n}", [P, 1024]) for n in range(2)]
        po = pb("po", [P, 512])
        pmisc = pb("pmisc", [P, 512])

        attn_in, router_in, cond_in, wmod_in = sem("attn_in"), sem("router_in"), sem("cond_in"), sem("wmod_in")
        expert_in, pads_out, mod_out = sem("expert_in"), sem("pads_out"), sem("mod_out")
        mod_in, mods_in = sem("mod_in"), sem("mods_in")
        consts_made, pool_done, dve_done = sem("consts_made"), sem("pool_done"), sem("dve_done")
        pool_passed = sem("pool_passed")
        setup_pe, setup_dve, setup_act = sem("setup_pe"), sem("setup_dve"), sem("setup_act")
        x_in, xr_in = sem("x_in"), [sem(f"xr_in{n}") for n in range(4)]
        veps_made, rstd_made, shift_made, xn_made = sem("veps_made"), sem("rstd_made"), sem("shift_made"), sem("xn_made")
        mod_now_made = sem("mod_now_made")
        tp_full, tp_free = [sem(f"tp_full{n}") for n in range(2)], [sem(f"tp_free{n}") for n in range(2)]
        sc_full, sc_free = [sem(f"sc_full{n}") for n in range(2)], [sem(f"sc_free{n}") for n in range(2)]
        po_full = sem("po_full")
        misc_full, misc_free = sem("misc_full"), sem("misc_free")
        hsum_made, wv_made = sem("hsum_made"), sem("wv_made")
        masked, exp_made, pm_made = sem("masked"), sem("exp_made"), sem("pm_made")
        x1_made, x1_stored = sem("x1_made"), [sem(f"x1_stored{n}") for n in range(2)]
        veps2_made, rstd2_made, shift2_made = sem("veps2_made"), sem("rstd2_made"), sem("shift2_made")
        xn2_made, h2_made = sem("xn2_made"), sem("h2_made")
        h2_rows_made = sem("h2_rows_made")
        routed_exp, exp_routed = sem("routed_exp"), sem("exp_routed")
        seen_made = sem("seen_made")
        chosen_made, slots_made, scattered = sem("chosen_made"), sem("slots_made"), sem("scattered")
        rows_sent = sem("rows_sent")
        high_made, low_made = sem("high_made"), sem("low_made")
        table_made, padded = sem("table_made"), sem("padded")
        hin_in = [sem(f"hin_in{n}") for n in range(UN)]
        hTp_full, hinT_high, hinT_made = sem("hTp_full"), sem("hinT_high"), sem("hinT_made")
        gu_full, act_made, fused_made = sem("gu_full"), sem("act_made"), sem("fused_made")
        fTp_full, fusedT_made, y_full, y_made = sem("fTp_full"), sem("fusedT_made"), sem("y_full"), sem("y_made")
        extra_made = sem("extra_made")
        y_out = [sem(f"y_out{n}") for n in range(UN)]
        gb_in = [sem(f"gb_in{n}") for n in range(UN)]
        out_done = sem("out_done")

        block = ctx.enter_context(nc.Block())

        wmod_sb = qv[:, 0:DC * 6 * D].rearrange("p (c n) -> p c n", c=DC)
        cond_sb = pen[0:B, 0:D]
        out_rows = out.rearrange("b s d -> (b s) d")
        x_rows = x.rearrange("b s d -> (b s) d")

        @block.sync
        def _(sp):
            sp.dma_start(cond_sb, cond[:, :]).then_inc(cond_in, 16)
            sp.dma_start(attn_sb[:, :, :], attn_w.rearrange("(c p) n -> p c n", p=P)).then_inc(attn_in, 16)
            sp.dma_start(xb[:, :, :], x[0, :, :].rearrange("(t p) d -> p t d", p=P)).then_inc(x_in, 16)
            sp.dma_start(wmod_sb, w_mod.rearrange("(c p) n -> p c n", p=P)).then_inc(wmod_in, 16)
            sp.dma_start(router_sb[:, :, :], router.rearrange("(c p) n -> p c n", p=P)).then_inc(router_in, 16)
            sp.wait_ge(setup_dve, 4)
            sp.dma_start(mod_hbm[:, :], mod_flat[:, 0:3, :].rearrange("b j d -> b (j d)")).then_inc(mod_out, 16)
            sp.dma_start(gb_hbm[:, :], mod_flat[:, 3, :]).then_inc(mod_out, 16)
            sp.wait_ge(mod_out, 32)
            for b0, b1, arrived in ((0, 1, mod_in), (1, B, mods_in)):
                sp.dma_start(mod_rows[:, b0:b1, :, :].rearrange("p b j d -> p (b j d)"),
                             mod_hbm[b0:b1, :].rearrange("b n -> (b n)").unsqueeze(0).to_broadcast([P, (b1 - b0) * 3 * D])
                             ).then_inc(arrived, 16)
            sp.wait_ge(consts_made, 2)
            sp.dma_start(rows_hbm[DUMMY:DUMMY + P, :], pad_row[:, :]).then_inc(pads_out, 16)
            sp.dma_start(sum_hbm[TOK:TOK + P, :], pad_row[:, 0:D]).then_inc(pads_out, 16)

            def batch(b, first, last):
                if not last:
                    for n in range(2):
                        sp.wait_ge(sc_full[n], nth(b, SC_USES, 1))
                    sp.dma_start(xb[:, :, :], x[bass.ds(b + 1, 1), :, :].rearrange("a (t p) d -> p (a t) d", p=P)
                                 ).then_inc(x_in, 16)
                for pos in range(-1, NT):
                    if pos + 1 < NT:
                        if not (first and pos + 1 < 4):
                            sp.wait_ge(x1_made, b * NT + (pos + 1 - 4 + 2))
                        tile = b * NT + ORDER[pos + 1]
                        sp.dma_start(xr[:, (pos + 1) % 4, :], x_rows[bass.ds(tile * P, P), :]
                                     ).then_inc(xr_in[(pos + 1) % 4], 16)
                    if pos >= 0:
                        sp.wait_ge(x1_made, nth(b, NT, pos + 1))
                        tile = b * NT + ORDER[pos]
                        sp.dma_start(sum_hbm[bass.ds(tile * P, P), :], x1[:, pos % 2, :]).then_inc(x1_stored[pos % 2], 16)
                        if first:
                            for e in range(pos * E // NT, (pos + 1) * E // NT):
                                for dst, src in ((raw[:, e, 0, :].rearrange("p (c n) -> p c n", c=DC), w_gate),
                                                 (raw[:, e, 1, :].rearrange("p (c n) -> p c n", c=DC), w_up),
                                                 (down_sb[:, e, :, :], w_down)):
                                    sp.dma_start(dst, src[e].rearrange("(c p) n -> p c n", p=P)).then_inc(expert_in, 16)

            batch(0, True, False)
            with sp.Fori(1, B - 1) as b:
                batch(b, False, False)
            batch(B - 1, False, True)

            def load_rows(t, n, at=None):
                if at is None:
                    at = sp.value_load(tile_row_i[0:1, bass.ds(t, 1)], min_val=0, max_val=DUMMY)
                sp.dma_start(hin[:, n, :], rows_hbm[bass.ds(at, P), :]).then_inc(hin_in[n], 16)

            sp.wait_ge(table_made, 1)
            firsts = [sp.value_load(tile_row_i[0:1, t:t + 1], min_val=0, max_val=DUMMY) for t in range(UN)]
            sp.wait_ge(h2_made, B * NT)
            sp.wait_ge(scattered, 16 * 2 * NT * (B - 1))
            for t in range(UN):
                load_rows(t, t, firsts[t])

            def refill(t, n):
                sp.wait_ge(hTp_full, t + 1)
                sp.wait_ge(extra_made, t + 1)
                load_rows(t + UN, n)

            for t in range(UN):
                refill(t, t)
            sp.wait_ge(table_made, 3)
            for e in range(E):
                at = sp.value_load(pad_i[0:1, e:e + 1], min_val=0, max_val=E * REG)
                sp.dma_start(rows_hbm[bass.ds(at, P), :], pad_row[:, :]).then_inc(padded, 16)
            with sp.Fori(1, FIRST // UN - 1) as i:
                for u in range(UN):
                    refill(UN * i + u, u)
            sp.wait_ge(padded, 16 * E)
            sp.wait_ge(scattered, 16 * 2 * NTT)
            sp.wait_ge(pads_out, 32)
            with sp.Fori(FIRST // UN - 1, TILES // UN - 1) as i:
                for u in range(UN):
                    refill(UN * i + u, u)
            for t in range(UN * (TILES // UN - 1), TILES - UN):
                refill(t, t % UN)

            for n in range(UN):
                sp.wait_ge(y_out[n], 16 * ((TILES + UN - 1 - n) // UN))
            sp.dma_start(out_rows, sum_hbm[0:TOK, :]).then_inc(out_done, 16)
            sp.wait_ge(out_done, 16)

        @block.gpsimd
        def _(pool):
            done = [0]

            def link(ins):
                done[0] += 1
                ins.then_inc(pool_done, 1)
                pool.wait_ge(pool_done, done[0])

            def passed():
                pool.sem_inc(pool_passed, 1)

            link(pool.memset(ident[:, :], 0.0))
            pool.affine_select(out=ident[:, :], in_=ident[:, :], compare_op=ALU.not_equal, fill=1.0, base=0,
                               pattern=[[-1, P]], channel_multiplier=1).then_inc(consts_made, 1)
            link(pool.memset(minus_half[:, :], -0.5))
            pool.wait_ge(veps_made, 1)
            pool.tensor_tensor(rstd[:, :], veps[:, :], minus_half[:, :], ALU.pow).then_inc(rstd_made, 1)
            link(pool.memset(upper[:, :], 1.0))
            link(pool.affine_select(out=upper[:, :], in_=upper[:, :], compare_op=ALU.is_ge, fill=0.0, base=0,
                                    pattern=[[1, P]], channel_multiplier=-1))
            link(pool.memset(before[:, :], 1.0))
            link(pool.affine_select(out=before[:, :], in_=before[:, :], compare_op=ALU.is_ge, fill=0.0, base=-1,
                                    pattern=[[1, P]], channel_multiplier=-1))
            link(pool.memset(ones[:, :], 1.0))
            link(pool.memset(neg_col[:, :], MASK_NEG))
            link(pool.memset(pm_rows[:, :, :].rearrange("p a b -> p (a b)"), 0.0))
            link(pool.memset(seen[:, :], 0.0))
            link(pool.memset(lower8[:, :, :].rearrange("p a b -> p (a b)"), 1.0))
            link(pool.affine_select(out=lower8[:, :, :], in_=lower8[:, :, :], compare_op=ALU.is_ge, fill=0.0, base=0,
                                    pattern=[[1, E], [-1, E]], channel_multiplier=0))
            link(pool.memset(pad_row[:, :], 0.0))
            for dst, pattern, n, base, per_row in (
                    (pad_row[:, D + 1:D + 2], [[0, 1]], 1, TOK, 1),
                    (region[:, :], [[REG, E]], E, 0, 0),
                    (choice_rank[:, :], [[-1, E]], E, E, 0),
                    (steps32[:, :], [[P, NTT]], NTT, 0, 0),
                    (token_of[:, :, 0], [[P, NTT]], NTT, 0, 1),
                    (token_of[:, :, 1], [[1, B], [0, NT]], NTT, 0, 0)):
                link(pool.iota(int_tmp[:, 0:n], pattern=pattern, base=base, channel_multiplier=per_row))
                link(pool.tensor_copy(dst, int_tmp[:, 0:n]))
            link(pool.iota(int_tmp[0:1, 0:TILES], pattern=[[1, TILES]], base=0, channel_multiplier=0))
            link(pool.tensor_copy(tile_no[:, :], int_tmp[0:1, 0:TILES]))
            pool.nop().then_inc(consts_made, 1)
            pool.wait_ge(mod_in, 16)
            pool.wait_ge(attn_in, 16)

            def mod_row(b, n):
                return mod_rows[:, bass.ds(b, 1), n, :].rearrange("p a d -> p (a d)")

            def scale_wv(b):
                for c in range(DC):
                    ins = pool.tensor_tensor(wv_sb[:, c, :], attn_sb[:, c, 2 * D:3 * D], mod_row(b, 0), ALU.mult)
                ins.then_inc(wv_made, 1)

            def send_rows(b, c, tiles):
                if 0 in tiles:
                    if c == 0:
                        pool.wait_ge(h2_rows_made, nth(b, 3, 2))
                        passed()
                        pool.wait_ge(slots_made, nth(b, 1, 0))
                    else:
                        pool.wait_ge(scattered, b * (16 * 2 * NT) + 16 * NT)
                    passed()
                    link(pool.tensor_copy(h2_rows[:, :, D:D + 3], extra[:, c, :, :]))
                for t in tiles:
                    pool.indirect_dma_start(
                        out=rows_hbm[:, :], out_offset=bass.IndirectOffsetOnAxis(ap=slot_i[:, c, t:t + 1], axis=0),
                        in_=h2_rows[:, t, :], in_offset=None).then_inc(scattered, 16)

            def all_sent(b):
                pool.wait_ge(scattered, b * (16 * 2 * NT) + 16 * 2 * NT)
                passed()
                pool.sem_inc(rows_sent, 1)

            def inverse_deviation(b, pos):
                pool.wait_ge(veps2_made, nth(b, NT, pos))
                pool.tensor_tensor(rstd2[:, pos % 2:pos % 2 + 1], veps2[:, pos % 2:pos % 2 + 1],
                                   minus_half[:, 0:1], ALU.pow).then_inc(rstd2_made, 1)

            def modulate_h2(b, pos):
                pool.wait_ge(xn2_made, nth(b, NT, pos + 2))
                passed()
                link(pool.tensor_tensor(h2[:, ORDER[pos], :], h2[:, ORDER[pos], :], mod_row(b, 2), ALU.mult))
                pool.tensor_tensor(h2[:, ORDER[pos], :], h2[:, ORDER[pos], :], mod_row(b, 1), ALU.add
                                   ).then_inc(h2_made, 1)

            def low_part(n):
                pool.wait_ge(high_made, n + 1)
                pool.tensor_tensor(low[:, n // 2, n % 2, :], raw[:, n // 2, n % 2, :], high[:, n // 2, n % 2, :].bitcast(fp32),
                                   ALU.subtract).then_inc(low_made, 1)

            def batch(b, first, last):
                pool.sem_clear(pool_done)
                done[0] = 0
                for k in range(1, NT):
                    if k == 2 and not last:
                        pool.wait_ge(veps_made, nth(b + 1, 1, 0))
                        pool.tensor_tensor(rstd[:, :], veps[:, :], minus_half[:, :], ALU.pow).then_inc(rstd_made, 1)
                    inverse_deviation(b, k - 1)
                    if k == 2 and first:
                        pool.wait_ge(mods_in, 16)
                    if k == 2 and not last:
                        pool.wait_ge(misc_full, MISCU.full(b, "vsum"))
                        passed()
                        scale_wv(b + 1)
                    if k >= 3:
                        modulate_h2(b, k - 3)
                    if last and k in (3, 4):
                        low_part(POOL_LOW[k - 3])
                    if k >= 5 and not first and not (last and k == NT - 1):
                        send_rows(b - 1, (k - 5) // 2, range(((k - 5) % 2) * NT // 2, ((k - 5) % 2 + 1) * NT // 2))
                modulate_h2(b, NT - 3)
                inverse_deviation(b, NT - 1)
                for pos in (NT - 2, NT - 1):
                    modulate_h2(b, pos)
                if not first:
                    send_rows(b - 1, 1, range(0 if last else NT // 2, NT))
                    if last:
                        low_part(POOL_LOW[2])
                    all_sent(b - 1)

            scale_wv(0)
            batch(0, True, False)
            with pool.Fori(1, B - 1) as b:
                batch(b, False, False)
            batch(B - 1, False, True)
            pool.sem_clear(pool_done)
            done[0] = 0
            for n in POOL_LOW[3:]:
                low_part(n)

            def take_extra(t, n, arrived):
                pool.wait_ge(hin_in[n], arrived)
                passed()
                pool.tensor_copy(row_weight[:, n, :], hin[:, n, D:D + 1])
                pool.tensor_copy(place_i[:, n, :], hin[:, n, D + 1:D + 3]).then_inc(extra_made, 1)

                pool.wait_ge(extra_made, t + 1)
                passed()
                pool.indirect_dma_start(
                    out=gb_rows[:, n, :], out_offset=None, in_=gb_hbm[:, :],
                    in_offset=bass.IndirectOffsetOnAxis(ap=place_i[:, n, 1:2], axis=0)).then_inc(gb_in[n], 16)

            def send_y(t, n, sent=None):
                pool.wait_ge(y_made, t + 1)
                passed()
                if sent is not None:
                    pool.wait_ge(y_out[(n - 1) % UN], sent)
                    passed()
                pool.indirect_dma_start(
                    out=sum_hbm[:, :], out_offset=bass.IndirectOffsetOnAxis(ap=place_i[:, n, 0:1], axis=0),
                    in_=y_sb[:, n, :], in_offset=None, compute_op=ALU.add).then_inc(y_out[n], 16)

            for n in range(2):
                pool.wait_ge(x1_stored[n], 16 * (NTT // 2) + 16)
            pool.wait_ge(pads_out, 32)
            pool.wait_ge(h2_rows_made, 3 * B)
            for t in range(UN):
                take_extra(t, t, 16)
            send_rows(B - 1, 0, range(NT))
            send_y(0, 0)

            def in_turn(i, u):
                pool.wait_ge(y_out[u], 16 * i + 16)
                passed()
                take_extra(UN * i + UN + u, u, 16 * i + 32)
                send_y(UN * i + 1 + u, (u + 1) % UN)

            for u in range(UN):
                in_turn(0, u)
                send_rows(B - 1, 1, range(u * NT // UN, (u + 1) * NT // UN))
            with pool.Fori(1, TILES // UN - 1) as i:
                for u in range(UN):
                    in_turn(i, u)
            for t in range(TILES // UN * UN, TILES):
                pool.wait_ge(y_out[t % UN], 16 * (t // UN))
                take_extra(t, t % UN, 16 * (t // UN + 1))
                send_y(t - UN + 1, (t + 1) % UN)
            for t in range(TILES - UN + 1, TILES):
                send_y(t, t % UN, 16 * ((t - 1) // UN + 1))

        @block.scalar
        def _(act):
            act.wait_ge(setup_pe, 1)
            act.activation(silu_c[:, :, :].rearrange("p c b -> p (c b)"), pmisc[:, 0:DC * B], ACT.Silu
                           ).then_inc(setup_act, 1)

            def normalise(b, tiles):
                act.wait_ge(shift_made, nth(b, 1, 0))
                for t in tiles:
                    act.activation(xb[:, t, :], xb[:, t, :], ACT.Identity, bias=shift[:, t:t + 1],
                                   scale=rstd[:, t:t + 1]).then_inc(xn_made, 1)

            normalise(0, range(NT))
            act.wait_ge(consts_made, 2)

            def h2T_out(b, it, pos):
                act.wait_ge(tp_full[TPU.buf(it, ("h", pos))], TPU.full(it, ("h", pos)))
                act.copy(h2T[:, pos % 2, :], tp[TPU.buf(it, ("h", pos))][:, 0:D]
                         ).then_inc(tp_free[TPU.buf(it, ("h", pos))], 1)

            def route_exp(b, n):
                act.wait_ge(routed_exp, nth(b, 2, n))
                flat = rs[2][:, :] if n else rt[0][:, :, :].rearrange("p t e -> p (t e)")
                act.activation(flat, flat, ACT.Exp).then_inc(exp_routed, 1)

            def high_part(n):
                act.copy(high[:, n // 2, n % 2, :], raw[:, n // 2, n % 2, :]).then_inc(high_made, 1)

            def ranks_out(it, counts):
                n = NT + 1 if counts else NT
                act.wait_ge(misc_full, MISCU.full(it, "rank"))
                act.copy(rank_sb[:, 0:n, :].rearrange("p t e -> p (t e)"), pmisc[:, 0:n * E]).then_inc(misc_free, 1)

            def normalise_x1(b, pos):
                act.wait_ge(shift2_made, nth(b, NT, pos))
                act.activation(h2[:, ORDER[pos], :], x1[:, pos % 2, :], ACT.Identity,
                               bias=shift2[:, pos % 2:pos % 2 + 1], scale=rstd2[:, pos % 2:pos % 2 + 1]
                               ).then_inc(xn2_made, 1)

            def copy_outer_rows(b):
                act.wait_ge(h2_made, nth(b, NT, NT // 2 - 1))
                act.wait_ge(rows_sent, nth(b, 1, 0))
                for t in (0, NT - 2):
                    act.copy(h2_rows[:, t:t + 2, 0:D], h2[:, t:t + 2, :]).then_inc(h2_rows_made, 1)

            def copy_inner_rows(b):
                act.wait_ge(h2_made, nth(b, NT, NT - 1))
                act.copy(h2_rows[:, 2:NT - 2, 0:D], h2[:, 2:NT - 2, :]).then_inc(h2_rows_made, 1)

            def batch(b, first, last):
                act.wait_ge(mod_now_made, nth(b, 1, 0))
                for half in range(2):
                    act.wait_ge(sc_full[0], nth(b, SC_USES, half))
                    act.activation(hT[:, 0, half * HALF:(half + 1) * HALF], sc[0][:, half * HALF:(half + 1) * HALF],
                                   ACT.Identity, bias=mod_now[:, 0:1], scale=mod_now[:, DC:DC + 1]
                                   ).then_inc(sc_free[0], 1)
                if not first:
                    normalise_x1(b - 1, NT - 2)
                    h2T_out(b - 1, b, 4)
                act.wait_ge(sc_full[0], nth(b, SC_USES, 2))
                act.copy(qT[:, 0, :], sc[0][:, :]).then_inc(sc_free[0], 1)
                if not first:
                    normalise_x1(b - 1, NT - 1)
                    h2T_out(b - 1, b, 5)

                def v_out(i):
                    n = TPU.buf(b, ("v", i))
                    act.wait_ge(tp_full[n], TPU.full(b, ("v", i)))
                    act.copy(v_sb[:, 2 * i:2 * i + 2, :].rearrange("p t d -> p (t d)"), tp[n][:, :]
                             ).then_inc(tp_free[n], 1)

                def exponentials(pos):
                    qi = ORDER[pos]
                    w = (NT - qi) * P
                    act.wait_ge(masked, nth(b, NT, pos))
                    act.activation(prob[:, pos % 2, 0:w], prob[:, pos % 2, 0:w], ACT.Exp,
                                   scale=-1.0, bias=negmax[:, pos:pos + 1], accum_out=rowsum[:, pos:pos + 1]).then_inc(exp_made, 1)
                    if qi > 0:
                        act.activation(pm_rows[:, pos, 0:qi], negmax[:, pos:pos + 1].to_broadcast([P, qi]),
                                       ACT.Exp, bias=neg_col[:, :]).then_inc(pm_made, 1)

                v_out(0)
                v_out(1)
                if not first:
                    h2T_out(b - 1, b, 6)
                exponentials(0)
                v_out(2)
                v_out(3)
                if not first:
                    copy_outer_rows(b - 1)
                    h2T_out(b - 1, b, 7)
                for k in range(NT):
                    if k == 4 and not first:
                        ranks_out(b, last)
                    for g, n in groups_of(k):
                        u = TPU.buf(b, ("p", k, g))
                        act.wait_ge(tp_full[u], TPU.full(b, ("p", k, g)))
                        act.copy(probT[:, k % 2, g * P:(g + n) * P], tp[u][:, 0:n * P]).then_inc(tp_free[u], 1)
                    if ORDER[k] > 0:
                        act.wait_ge(misc_full, MISCU.full(b, ("pm", k)))
                        act.copy(pmT[:, k % 2, :], pmisc[0:NT, 0:P]).then_inc(misc_free, 1)
                    if k + 1 < NT:
                        exponentials(k + 1)
                    if k == 1 and not first:
                        copy_inner_rows(b - 1)
                    if k >= 2:
                        normalise_x1(b, k - 2)
                    if k >= NT - OWN_H:
                        h2T_out(b, b, k - (NT - OWN_H))
                    if k in (1, 3) and not first:
                        route_exp(b - 1, k // 2)
                    if k >= 4 and not last:
                        normalise(b + 1, range((k - 4) * NT // 4, (k - 3) * NT // 4))
                    if last and k == 1:
                        act.wait_ge(expert_in, 16 * 3 * E)
                    if last and 1 <= k < 5:
                        high_part(k - 1)
                    if last and k == 7:
                        high_part(4)
                        high_part(5)

            batch(0, True, False)
            with act.Fori(1, B - 1) as b:
                batch(b, False, False)
            batch(B - 1, False, True)

            normalise_x1(B - 1, NT - 2)
            h2T_out(B - 1, B, 4)
            act.wait_ge(po_full, B * NT)
            high_part(6)
            normalise_x1(B - 1, NT - 1)
            for n, pos in enumerate((5, 6, 7)):
                high_part(7 + n)
                h2T_out(B - 1, B, pos)
            high_part(10)
            route_exp(B - 1, 0)
            for n in (11, 12, 13):
                high_part(n)
            route_exp(B - 1, 1)
            ranks_out(B, True)
            for n in range(14, 2 * E):
                high_part(n)
            copy_outer_rows(B - 1)
            copy_inner_rows(B - 1)

            def silu(t, par):
                act.wait_ge(gu_full, t + 1)
                act.activation(act_sb[:, par, :], sc[0][:, par * F:(par + 1) * F], ACT.Silu).then_inc(act_made, 1)

            def fused_out(t, par):
                act.wait_ge(fTp_full, t + 1)
                act.copy(fusedT[:, par, :], tp[1][:, :]).then_inc(fusedT_made, 1)

            act.wait_ge(h2_rows_made, 3 * B)
            silu(0, 0)
            silu(1, 1)
            fused_out(0, 0)
            with act.Fori(0, LOOPS) as i:
                for u in range(UN):
                    silu(UN * i + 2 + u, u % 2)
                    fused_out(UN * i + 1 + u, (1 + u) % 2)
            silu(TILES - 1, (TILES - 1) % 2)
            fused_out(TILES - 2, (TILES - 2) % 2)
            fused_out(TILES - 1, (TILES - 1) % 2)

        @block.vector
        def _(dve):
            done = [0]

            def link(ins):
                done[0] += 1
                ins.then_inc(dve_done, 1)
                dve.wait_ge(dve_done, done[0])

            def counted(ins):
                done[0] += 1
                ins.then_inc(dve_done, 1)

            for s, n in ((tp_free[0], 1), (tp_free[1], 1), (xn2_made, 2), (x1_stored[0], 16),
                         (x1_stored[1], 16)):
                dve.nop().then_inc(s, n)

            def ln_stats(b):
                dve.wait_ge(x_in, b * 16 + 16)
                for t in range(NT):
                    counted(dve.bn_stats(stats[:, t, :], xb[:, t, :]))
                dve.wait_ge(dve_done, done[0])
                for t in range(NT):
                    counted(dve.bn_aggr(mv[:, t, :], stats[:, t, :]))
                dve.wait_ge(dve_done, done[0])
                dve.tensor_scalar(veps[:, :], mv[:, :, 1], EPS, None, ALU.add).then_inc(veps_made, 1)

            def ln_shift(b):
                dve.wait_ge(rstd_made, nth(b, 1, 0))
                dve.scalar_tensor_tensor(out=shift[:, :], in0=mv[:, :, 0], scalar=-1.0, in1=rstd[:, :],
                                         op0=ALU.mult, op1=ALU.mult).then_inc(shift_made, 1)

            dve.wait_ge(setup_pe, 2)
            wT = hT
            dve.tensor_copy(wT[:, 0, :], sc[0][:, :]).then_inc(setup_dve, 1)
            ln_stats(0)
            dve.wait_ge(setup_pe, 3)
            dve.tensor_scalar(qk_sb[:, :, :].rearrange("p c d -> p (c d)"), po[:, :], -float(D) ** -0.5, None, ALU.mult
                              ).then_inc(setup_dve, 1)
            ln_shift(0)
            dve.wait_ge(setup_pe, 4)
            cols = mod_cols[:, :, :].rearrange("p j b -> p (j b)")
            link(dve.tensor_copy(cols, pmisc[:, 0:2 * DC * B]))
            n = DC * B
            dve.tensor_scalar(cols[:, n:2 * n], cols[:, n:2 * n], 1.0, None, ALU.add).then_inc(setup_dve, 1)
            dve.wait_ge(setup_dve, 3)
            for s in (x1_made, misc_free, rows_sent, seen_made):
                dve.nop().then_inc(s, 1)

            def gates():
                dve.wait_ge(setup_pe, 5)
                for n in range(2):
                    link(dve.tensor_copy(mod_flat[:, 2 * n:2 * n + 2, :].rearrange("b j d -> b (j d)"), tp[n][0:B, :]))
                link(dve.tensor_scalar(mod_flat[:, 2, :], mod_flat[:, 2, :], 1.0, None, ALU.add))
                ga_gb = mod_flat[:, 0:4:3, :]
                sign, size = (pen[0:B, n * 2 * D:(n + 1) * 2 * D].rearrange("p (j d) -> p j d", j=2) for n in range(2))
                link(dve.tensor_scalar(sign, ga_gb, 0.0, 2.0, ALU.is_ge, ALU.mult))
                link(dve.tensor_scalar(sign, sign, 1.0, None, ALU.subtract))
                link(dve.tensor_scalar(size, ga_gb, -1.0, None, ALU.mult))
                link(dve.tensor_tensor(size, ga_gb, size, ALU.max))
                link(dve.tensor_scalar(size, size, 0.25, None, ALU.max))
                dve.tensor_tensor(ga_gb, size, sign, ALU.mult).then_inc(setup_dve, 1)
                dve.wait_ge(setup_dve, 4)

            dve.wait_ge(consts_made, 2)

            def mask(b, pos):
                qi = ORDER[pos]
                w = (NT - qi) * P
                buf = sc[pos % 2]
                dve.wait_ge(sc_full[pos % 2], nth(b, SC_USES, 3 + pos // 2))
                if pos >= 2:
                    use = ("p", pos - 2, groups_of(pos - 2)[-1][0])
                    dve.wait_ge(tp_full[TPU.buf(b, use)], TPU.full(b, use))
                link(dve.tensor_tensor(buf[:, 0:P], buf[:, 0:P], upper[:, :], ALU.mult))
                link(dve.tensor_scalar(pen[:, 0:w], buf[:, 0:w], 0.0, -MASK_NEG, ALU.is_equal, ALU.mult))
                dve.tensor_tensor_reduce(out=prob[:, pos % 2, 0:w], in0=buf[:, 0:w], in1=pen[:, 0:w], scale=1.0,
                                         scalar=-MASK_NEG if qi > 0 else -LOWEST, op0=ALU.add, op1=ALU.min,
                                         accum_out=negmax[:, pos:pos + 1]).then_inc(masked, 1)

            def normaliser(b, k):
                qi = ORDER[k]
                dve.wait_ge(exp_made, nth(b, NT, k))
                if qi > 0:
                    dve.wait_ge(pm_made, nth(b, NT - 1, sum(1 for q in ORDER[:k] if q > 0)))
                    link(dve.scalar_tensor_tensor(out=rowsum[:, k:k + 1], in0=pm_rows[:, k, 0:1],
                                                  scalar=float(P * qi), in1=rowsum[:, k:k + 1],
                                                  op0=ALU.mult, op1=ALU.add))
                link(dve.reciprocal(rinv[:, k:k + 1], rowsum[:, k:k + 1]))

            def residual(b, pos):
                dve.wait_ge(po_full, nth(b, NT, pos))
                dve.wait_ge(xn2_made, nth(b, NT, pos))
                dve.wait_ge(x1_stored[pos % 2], b * (8 * NT) + 16 * (pos // 2 + 1))
                dve.wait_ge(xr_in[pos % 4], b * 32 + 16 * (pos // 4 + 1))
                dve.scalar_tensor_tensor(out=x1[:, pos % 2, :], in0=po[:, 0:D], scalar=rinv[:, pos:pos + 1],
                                         in1=xr[:, pos % 4, :], op0=ALU.mult, op1=ALU.add).then_inc(x1_made, 1)
                dve.wait_ge(x1_made, b * NT + (pos + 2))
                link(dve.bn_stats(stats2[:, :], x1[:, pos % 2, :]))
                link(dve.bn_aggr(mv2[:, pos % 2, :], stats2[:, :]))
                dve.tensor_scalar(veps2[:, pos % 2:pos % 2 + 1], mv2[:, pos % 2, 1:2], EPS, None, ALU.add
                                  ).then_inc(veps2_made, 1)

            def shift_of(b, pos):
                dve.wait_ge(rstd2_made, nth(b, NT, pos))
                n = pos % 2
                dve.scalar_tensor_tensor(out=shift2[:, n:n + 1], in0=mv2[:, n, 0:1], scalar=-1.0, in1=rstd2[:, n:n + 1],
                                         op0=ALU.mult, op1=ALU.mult).then_inc(shift2_made, 1)

            def logits_out(it, pos):
                dve.wait_ge(misc_full, MISCU.full(it, ("lg", pos)))
                dve.tensor_copy(lg[:, ORDER[pos], :], pmisc[:, 0:E]).then_inc(misc_free, 1)

            def low_part(n):
                dve.wait_ge(high_made, n + 1)
                dve.tensor_tensor(low[:, n // 2, n % 2, :], raw[:, n // 2, n % 2, :], high[:, n // 2, n % 2, :].bitcast(fp32),
                                  ALU.subtract).then_inc(low_made, 1)

            def batch(b, first, last):
                done[0] = 0
                dve.sem_clear(dve_done)
                dve.tensor_copy(mod_now[:, :], mod_cols[:, :, bass.ds(b, 1)].rearrange("p j a -> p (j a)")
                                ).then_inc(mod_now_made, 1)
                dve.wait_ge(mod_now_made, nth(b, 1, 0))
                for half in range(2):
                    dve.wait_ge(sc_full[1], nth(b, SC_USES, half))
                    dve.tensor_scalar(hT[:, 1, half * HALF:(half + 1) * HALF], sc[1][:, half * HALF:(half + 1) * HALF],
                                      mod_now[:, DC + 1:DC + 2], mod_now[:, 1:2], ALU.mult, ALU.add
                                      ).then_inc(sc_free[1], 1)
                if first:
                    gates()
                if not first:
                    shift_of(b - 1, NT - 2)
                    residual(b - 1, NT - 1)
                    logits_out(b, 3)
                dve.wait_ge(sc_full[1], nth(b, SC_USES, 2))
                dve.tensor_copy(qT[:, 1, :], sc[1][:, :]).then_inc(sc_free[1], 1)
                if not first:
                    shift_of(b - 1, NT - 1)
                    logits_out(b, 4)
                mask(b, 0)
                dve.wait_ge(sc_free[0], b * SC_FREED + 2)
                dve.tensor_reduce(hsum[:, :, :].rearrange("p c t -> p (c t)"),
                                  hT[:, :, :].rearrange("p c (t s) -> p (c t) s", s=P), AX.X, ALU.add
                                  ).then_inc(hsum_made, 1)
                if not first:
                    logits_out(b, 5)
                if not first:
                    logits_out(b, 6)
                mask(b, 1)
                dve.wait_ge(misc_full, MISCU.full(b, "vsum"))
                dve.tensor_copy(vsum[:, :], pmisc[0:NT, 0:D]).then_inc(misc_free, 1)
                dve.wait_ge(misc_free, MISCU.read(b, "vsum"))
                normaliser(b, 0)
                if not first:
                    logits_out(b, 7)
                    route_logits(b - 1, b)
                if not last:
                    ln_stats(b + 1)
                for k in range(1, NT):
                    if k + 1 < NT:
                        mask(b, k + 1)
                    if k >= NT - OWN_LG:
                        logits_out(b, k - (NT - OWN_LG))
                    if k >= 2:
                        shift_of(b, k - 2)
                    residual(b, k - 1)
                    normaliser(b, k)
                    if k == 2 and not first:
                        for c in range(2):
                            route_choice(b - 1, c)
                    if k == 3 and not last:
                        ln_shift(b + 1)
                    if k == 4 and not first:
                        route_slots(b - 1, b)
                        if last:
                            low_part(2)
                    if k == 5 and last:
                        first_tiles(0)
                    if k == 6 and last:
                        first_tiles(1)
                    if k == 7 and last:
                        low_part(3)

            counts = rank_sb[:, NT, :]

            def tiles_in(rows, into, ends, grid):
                g3 = grid[:, 0, 0:E * NTT].rearrange("p (e m) -> p e m", e=E)
                g8 = grid[:, 0, 0:E * E].rearrange("p (a b) -> p a b", a=E)
                link(dve.tensor_tensor(g3, rows.unsqueeze(2).to_broadcast([P, E, NTT]),
                                       steps32[:, :].unsqueeze(1).to_broadcast([P, E, NTT]), ALU.is_gt))
                link(dve.tensor_reduce(into, g3, AX.X, ALU.add))
                link(dve.tensor_tensor(g8, lower8[:, :, :], into.unsqueeze(1).to_broadcast([P, E, E]), ALU.mult))
                link(dve.tensor_reduce(ends, g8, AX.X, ALU.add))

            def entries(t0, t1, ends, at0, t_less, grid):
                n = t1 - t0
                ge = grid[0:1, 0, 0:n * E].rearrange("p (t e) -> p t e", e=E)
                gs = grid[0:1, 1, 0:n * E].rearrange("p (t e) -> p t e", e=E)
                ex, row = tile_exp[:, t0:t1], tile_row[:, t0:t1]
                link(dve.tensor_tensor(ge, tile_no[:, t0:t1].unsqueeze(2).to_broadcast([1, n, E]),
                                       ends.unsqueeze(1).to_broadcast([1, n, E]), ALU.is_ge))
                link(dve.tensor_tensor(gs, ge, jump[0:1, :].unsqueeze(1).to_broadcast([1, n, E]), ALU.mult))
                link(dve.tensor_reduce(ex, ge, AX.X, ALU.add))
                link(dve.tensor_reduce(row, gs, AX.X, ALU.add))
                link(dve.scalar_tensor_tensor(out=row, in0=tile_no[:, t0:t1], scalar=float(P), in1=row,
                                              op0=ALU.mult, op1=ALU.add))
                if t_less:
                    link(dve.tensor_scalar(row, row, float(-P * t_less), None, ALU.add))
                    link(dve.scalar_tensor_tensor(out=row, in0=at0.to_broadcast([1, n]), scalar=float(P), in1=row,
                                                  op0=ALU.mult, op1=ALU.add))
                link(dve.tensor_scalar(row, row, float(DUMMY), None, ALU.min))
                link(dve.tensor_copy(tile_row_i[:, t0:t1], row))
                link(dve.tensor_scalar(ex, ex, float(E - 1), None, ALU.min))
                dve.tensor_copy(tile_exp_i[:, t0:t1], ex).then_inc(table_made, 1)

            def first_tiles(part):
                if part == 1:
                    entries(0, FIRST, full_end[0:1, 1:E + 1], None, 0, grids[0])
                    return
                dve.wait_ge(misc_free, MISCU.read(B - 1, "rank"))
                link(dve.tensor_scalar(full_count[:, :], counts, float(P - 1), None, ALU.subtract))
                link(dve.memset(full_end[:, 0:1], 0.0))
                link(dve.memset(full_of[:, E:E + 1], 0.0))
                tiles_in(full_count[:, :], full_of[:, 0:E], full_end[:, 1:E + 1], grids[0])
                link(dve.tensor_scalar(full_end[:, 1:E + 1], full_end[:, 1:E + 1], float(FIRST), None, ALU.min))
                link(dve.tensor_tensor(full_of[:, 0:E], full_end[:, 1:E + 1], full_end[:, 0:E], ALU.subtract))
                link(dve.tensor_scalar(jump[:, :], full_of[:, 0:E], float(-P), float(REG), ALU.mult, ALU.add))

            def rest_tiles(part):
                if part == 0:
                    tiles_in(counts, tiles_of[:, :], rest_end[:, :], grids[1])
                    link(dve.tensor_tensor(pad_at[:, :], counts[0:1, :], region[0:1, :], ALU.add))
                    dve.tensor_copy(pad_i[:, :], pad_at[:, :]).then_inc(table_made, 1)
                    return
                link(dve.tensor_tensor(rest_end[:, :], rest_end[:, :], full_end[:, 1:E + 1], ALU.subtract))
                link(dve.tensor_scalar(rest_end[:, :], rest_end[:, :], float(FIRST), None, ALU.add))
                link(dve.tensor_tensor(jump[:, :], full_of[:, 1:E + 1], tiles_of[:, :], ALU.subtract))
                link(dve.tensor_scalar(jump[:, :], jump[:, :], float(P), float(REG), ALU.mult, ALU.add))
                entries(FIRST, TILES, rest_end[0:1, :], full_of[0:1, 0:1], FIRST, grids[1])

            p3, t3, q3 = (r[:, :, :] for r in rt)
            s0, s1, s2, s3 = (r[:, :] for r in rs)
            rank3 = choice_rank[:, :].unsqueeze(1).to_broadcast([P, NT, E])
            region3 = region[:, :].unsqueeze(1).to_broadcast([P, NT, E])

            def wide(s):
                return s.unsqueeze(2).to_broadcast([P, NT, E])

            def route_logits(b, it):
                dve.wait_ge(misc_free, MISCU.read(it, ("lg", NT - 1)))
                link(dve.tensor_reduce(s0, lg[:, :, :], AX.X, ALU.max))
                dve.tensor_tensor(p3, lg[:, :, :], wide(s0), ALU.subtract).then_inc(routed_exp, 1)

            def route_choice(b, c):
                if c == 0:
                    dve.wait_ge(exp_routed, nth(b, 2, 0))
                    link(dve.tensor_reduce(s0, p3, AX.X, ALU.add))
                    link(dve.reciprocal(s1, s0))
                    link(dve.tensor_tensor(p3, p3, wide(s1), ALU.mult))
                top, one_hot = (s0, s1)[c], pick[:, c, :, :]
                link(dve.tensor_reduce(top, p3, AX.X, ALU.max))
                link(dve.tensor_tensor(t3, p3, wide(top), ALU.is_equal))
                link(dve.tensor_tensor(t3, t3, rank3, ALU.mult))
                link(dve.tensor_reduce(s3, t3, AX.X, ALU.max))
                link(dve.tensor_tensor(one_hot, t3, wide(s3), ALU.is_equal))
                if c == 0:
                    link(dve.scalar_tensor_tensor(out=p3, in0=one_hot, scalar=-2.0, in1=p3, op0=ALU.mult, op1=ALU.add))
                    return
                dve.tensor_tensor(chosen[:, :, :], pick[:, 0, :, :], pick[:, 1, :, :], ALU.add).then_inc(chosen_made, 1)
                dve.tensor_tensor(s2, s1, s0, ALU.subtract).then_inc(routed_exp, 1)

            def route_slots(b, it):
                dve.wait_ge(rows_sent, nth(b, 1, 0))
                for c in range(2):
                    counted(dve.tensor_copy(extra[:, c, :, 1:3], token_of[:, bass.ds(b * NT, NT), :]))
                dve.wait_ge(misc_free, MISCU.read(it, "rank"))
                counted(dve.tensor_tensor(t3, rank_sb[:, 0:NT, :], region3, ALU.add))
                dve.wait_ge(exp_routed, nth(b, 2, 1))
                link(dve.tensor_scalar(s3, s2, 1.0, None, ALU.add))
                link(dve.reciprocal(s0, s3))
                counted(dve.tensor_copy(extra[:, 0, :, 0], s0))
                counted(dve.tensor_tensor(extra[:, 1, :, 0], s2, s0, ALU.mult))
                dve.wait_ge(dve_done, done[0])
                for c in range(2):
                    link(dve.tensor_tensor(q3, t3, pick[:, c, :, :], ALU.mult))
                    link(dve.tensor_reduce(slot[:, :], q3, AX.X, ALU.add))
                    ins = dve.tensor_copy(slot_i[:, c, :], slot[:, :])
                    if c == 0:
                        link(ins)
                ins.then_inc(slots_made, 1)
                link(dve.tensor_reduce(added[:, :], chosen[:, :, :].rearrange("p t e -> p e t"), AX.X, ALU.add))
                dve.tensor_tensor(seen[:, :], seen[:, :], added[:, :], ALU.add).then_inc(seen_made, 1)

            batch(0, True, False)
            with dve.Fori(1, B - 1) as b:
                batch(b, False, False)
            batch(B - 1, False, True)
            dve.sem_clear(dve_done)
            done[0] = 0

            shift_of(B - 1, NT - 2)
            residual(B - 1, NT - 1)
            logits_out(B, 3)
            shift_of(B - 1, NT - 1)
            logits_out(B, 4)
            low_part(4)
            logits_out(B, 5)
            low_part(5)
            logits_out(B, 6)
            low_part(6)
            logits_out(B, 7)
            route_logits(B - 1, B)
            low_part(7)
            route_choice(B - 1, 0)
            route_choice(B - 1, 1)
            for n in range(8, 2 * E):
                if n not in POOL_LOW:
                    low_part(n)

            for n in range(2):
                dve.wait_ge(x1_stored[n], 16 * (NTT // 2) + 16)

            def rows_out(t, par):
                dve.wait_ge(hTp_full, t + 1)
                dve.tensor_copy(hinT[:, par, 0, :], tp[0][:, 0:D]).then_inc(hinT_high, 1)
                dve.wait_ge(hinT_high, t + 1)
                dve.tensor_tensor(hinT[:, par, 1, :], tp[0][:, 0:D], hinT[:, par, 0, :].bitcast(fp32), ALU.subtract
                                  ).then_inc(hinT_made, 1)

            def product(t, par):
                dve.wait_ge(act_made, t + 1)
                dve.tensor_tensor(fused[:, par, :], act_sb[:, par, :], sc[1][:, par * F:(par + 1) * F], ALU.mult
                                  ).then_inc(fused_made, 1)

            def y_to_sbuf(t, n, sent, arrived):
                dve.wait_ge(extra_made, t + 1)
                dve.wait_ge(y_full, t + 1)
                if sent is not None:
                    dve.wait_ge(y_out[n], sent)
                dve.wait_ge(gb_in[n], arrived)
                dve.scalar_tensor_tensor(out=y_sb[:, n, :], in0=(po if n % 2 == 0 else pmisc)[:, 0:D],
                                         scalar=row_weight[:, n, :], in1=gb_rows[:, n, :],
                                         op0=ALU.mult, op1=ALU.mult).then_inc(y_made, 1)

            rows_out(0, 0)
            rows_out(1, 1)
            route_slots(B - 1, B)
            rest_tiles(0)
            product(0, 0)
            rows_out(2, 0)
            product(1, 1)

            def step(t, u, sent, arrived):
                product(t + 1, (u + 1) % 2)
                rows_out(t + 2, u % 2)
                y_to_sbuf(t - 1, (u - 1) % UN, sent, arrived)

            for t in range(1, UN + 1):
                step(t, t, None, 16)
                if t == 1:
                    rest_tiles(1)
            with dve.Fori(1, LOOPS) as i:
                for u in range(UN):
                    step(UN * i + 1 + u, u + 1, 16 * i, 16 * i + 16)
            product(TILES - 1, (TILES - 1) % 2)
            for t in range(TILES - 3, TILES):
                y_to_sbuf(t, t % UN, 16 * (t // UN), 16 * (t // UN + 1))

        @block.tensor
        def _(pe):
            pe.wait_ge(consts_made, 1)
            pe.wait_ge(cond_in, 16)
            for c in range(DC):
                mm = pe.transpose(pmisc[:, c * B:(c + 1) * B], cond_sb[:, c * P:(c + 1) * P], ident[0:B, 0:B])
            mm.then_inc(setup_pe, 1)
            pe.wait_ge(attn_in, 16)
            for j in range(2):
                for f in range(DC):
                    for c in range(DC):
                        o = (j * DC + f) * D + c * P
                        mm = pe.transpose(sc[0][:, o:o + P], attn_sb[:, c, j * D + f * P:j * D + (f + 1) * P], ident[:, :])
            mm.then_inc(setup_pe, 1)
            pe.wait_ge(setup_dve, 1)
            for i in range(DC):
                for f in range(DC):
                    mm = pe.matmul(po[:, i * D:(i + 1) * D], hT[:, 0, f * D + i * P:f * D + (i + 1) * P],
                                   hT[:, 0, (DC + f) * D:(DC + f + 1) * D], start=(f == 0), stop=(f == DC - 1))
            mm.then_inc(setup_pe, 1)
            pe.wait_ge(setup_act, 1)
            pe.wait_ge(wmod_in, 16)
            for j in range(2 * DC):
                for c in range(DC):
                    mm = pe.matmul(pmisc[:, j * B:(j + 1) * B], wmod_sb[:, c, j * P:(j + 1) * P], silu_c[:, c, :],
                                   start=(c == 0), stop=(c == DC - 1))
            mm.then_inc(setup_pe, 1)
            for half in range(2):
                for c in range(DC):
                    o = 2 * D + half * 512
                    mm = pe.matmul(tp[half][0:B, :], silu_c[:, c, :],
                                   wmod_sb[:, c, o:o + 512], start=(c == 0), stop=(c == DC - 1))
            mm.then_inc(setup_pe, 1)
            pe.wait_ge(router_in, 16)

            def h2_transposed(b, it, pos):
                u = ("h", pos)
                pe.wait_ge(h2_made, nth(b, NT, pos))
                pe.wait_ge(tp_free[TPU.buf(it, u)], TPU.full(it, u))
                for c in range(DC):
                    mm = pe.transpose(tp[TPU.buf(it, u)][:, c * P:(c + 1) * P], h2[:, ORDER[pos], c * P:(c + 1) * P],
                                      ident[:, :])
                mm.then_inc(tp_full[TPU.buf(it, u)], 1)

            def logits(it_h, it, pos):
                pe.wait_ge(tp_free[TPU.buf(it_h, ("h", pos))], TPU.read(it_h, ("h", pos)))
                pe.wait_ge(misc_free, MISCU.full(it, ("lg", pos)))
                for c in range(DC):
                    mm = pe.matmul(pmisc[:, 0:E], h2T[:, pos % 2, c * P:(c + 1) * P], router_sb[:, c, :],
                                   start=(c == 0), stop=(c == DC - 1))
                mm.then_inc(misc_full, 1)

            def scores(b, pos):
                qi = ORDER[pos]
                w = (NT - qi) * P
                if pos >= 2:
                    pe.wait_ge(masked, nth(b, NT, pos - 2))
                for o in range(0, w, 512):
                    n = min(512, w - o)
                    for c in range(DC):
                        mm = pe.matmul(sc[pos % 2][:, o:o + n], qT[:, c, qi * P:(qi + 1) * P],
                                       hT[:, c, qi * P + o:qi * P + o + n], start=(c == 0), stop=(c == DC - 1))
                mm.then_inc(sc_full[pos % 2], 1)

            def values(b, pos):
                qi = ORDER[pos]
                pe.wait_ge(x1_made, nth(b, NT, pos))
                for g, n in groups_of(pos):
                    u = ("p", pos, g)
                    pe.wait_ge(tp_free[TPU.buf(b, u)], TPU.read(b, u))
                    for i in range(n):
                        j = g + i
                        mm = pe.matmul(po[:, 0:D], probT[:, pos % 2, j * P:(j + 1) * P], v_sb[:, qi + j, :],
                                       start=(j == 0), stop=(j == NT - 1 - qi and qi == 0))
                if qi > 0:
                    pe.wait_ge(misc_free, MISCU.read(b, ("pm", pos)))
                    mm = pe.matmul(po[:, 0:D], pmT[:, pos % 2, :], vsum[:, :], start=False, stop=True)
                mm.then_inc(po_full, 1)

            def v_product(b, i):
                u = ("v", i)
                pe.wait_ge(tp_free[TPU.buf(b, u)], TPU.full(b, u))
                for t in (2 * i, 2 * i + 1):
                    for c in range(DC):
                        mm = pe.matmul(tp[TPU.buf(b, u)][:, (t % 2) * D:(t % 2 + 1) * D], hT[:, c, t * P:(t + 1) * P],
                                       wv_sb[:, c, :], start=(c == 0), stop=(c == DC - 1))
                mm.then_inc(tp_full[TPU.buf(b, u)], 1)

            def ranks(b, it, counts):
                pe.wait_ge(chosen_made, nth(b, 1, 0))
                pe.wait_ge(misc_free, MISCU.full(it, "rank"))
                pe.matmul(pmisc[:, 0:NT * E], before[:, :], chosen[:, :, :].rearrange("p t e -> p (t e)"),
                          start=True, stop=False)
                for n in range(1, NT):
                    pe.matmul(pmisc[:, n * E:NT * E], ones[:, :], chosen[:, 0:NT - n, :].rearrange("p t e -> p (t e)"),
                              start=False, stop=False)
                pe.wait_ge(seen_made, nth(b, 1, 0))
                n = NT + 1 if counts else NT
                if counts:
                    for t in range(NT):
                        pe.matmul(pmisc[:, NT * E:(NT + 1) * E], ones[:, :], chosen[:, t, :], start=False, stop=False)
                pe.matmul(pmisc[:, 0:n * E].rearrange("p (t e) -> p t e", e=E), ones[:, :],
                          seen[:, :].unsqueeze(1).to_broadcast([P, n, E]), start=False, stop=True).then_inc(misc_full, 1)

            def batch(b, first, last):
                if not first:
                    pe.wait_ge(masked, nth(b - 1, NT, NT - 1))
                for half in range(2):
                    for t in range(half * NT // 2, (half + 1) * NT // 2):
                        pe.wait_ge(xn_made, nth(b, NT, t))
                        for c in range(DC):
                            mm = pe.transpose(sc[c][:, t * P:(t + 1) * P], xb[:, t, c * P:(c + 1) * P], ident[:, :])
                            if t == (half + 1) * NT // 2 - 1:
                                mm.then_inc(sc_full[c], 1)
                if not first:
                    values(b - 1, NT - 1)
                for f in range(DC):
                    for c in range(DC):
                        pe.wait_ge(sc_free[c], b * SC_FREED + 2)
                    for half in range(2):
                        for c in range(DC):
                            mm = pe.matmul(sc[f][:, half * HALF:(half + 1) * HALF], qk_sb[:, c, f * P:(f + 1) * P],
                                           hT[:, c, half * HALF:(half + 1) * HALF], start=(c == 0), stop=(c == DC - 1))
                    mm.then_inc(sc_full[f], 1)
                    if not first:
                        h2_transposed(b - 1, b, 4 + f)
                        logits(b - 1 if f == 0 else b, b, 3 + f)
                if first:
                    for f in range(DC):
                        pe.wait_ge(sc_free[f], b * SC_FREED + 3)
                    scores(b, 0)
                    scores(b, 1)
                    pe.wait_ge(setup_dve, 4)
                pe.wait_ge(wv_made, nth(b, 1, 0))
                v_product(b, 0)
                v_product(b, 1)
                if not first:
                    h2_transposed(b - 1, b, 6)
                    for f in range(DC):
                        pe.wait_ge(sc_free[f], b * SC_FREED + 3)
                    scores(b, 0)
                    logits(b, b, 5)
                v_product(b, 2)
                v_product(b, 3)
                if not first:
                    scores(b, 1)
                if not first:
                    logits(b, b, 6)
                pe.wait_ge(hsum_made, nth(b, 1, 0))
                pe.wait_ge(misc_free, MISCU.full(b, "vsum"))
                for c in range(DC):
                    mm = pe.matmul(pmisc[0:NT, 0:D], hsum[:, c, :], wv_sb[:, c, :],
                                   start=(c == 0), stop=(c == DC - 1))
                mm.then_inc(misc_full, 1)
                if not first:
                    h2_transposed(b - 1, b, 7)
                for i in (2, 3):
                    pe.wait_ge(tp_free[TPU.buf(b, ("v", i))], TPU.read(b, ("v", i)))
                for k in range(NT):
                    qi = ORDER[k]
                    if 1 <= k and k + 1 < NT:
                        scores(b, k + 1)
                    if k == 4 and not first:
                        ranks(b - 1, b, last)
                    if k >= 1:
                        values(b, k - 1)
                    if k >= NT - OWN_LG:
                        logits(b, b, k - (NT - OWN_LG))
                    pe.wait_ge(exp_made, nth(b, NT, k))
                    for g, n in groups_of(k):
                        u = ("p", k, g)
                        pe.wait_ge(tp_free[TPU.buf(b, u)], TPU.full(b, u))
                        for i in range(n):
                            mm = pe.transpose(tp[TPU.buf(b, u)][:, i * P:(i + 1) * P],
                                              prob[:, k % 2, (g + i) * P:(g + i + 1) * P], ident[:, :])
                        mm.then_inc(tp_full[TPU.buf(b, u)], 1)
                    if k == 0 and not first:
                        logits(b, b, 7)
                    if qi > 0:
                        pe.wait_ge(pm_made, nth(b, NT - 1, sum(1 for q in ORDER[:k] if q > 0)))
                        pe.wait_ge(misc_free, MISCU.full(b, ("pm", k)))
                        pe.transpose(pmisc[0:NT, 0:P], pm_rows[:, k, :], ident[:, :]).then_inc(misc_full, 1)
                    if k >= NT - OWN_H:
                        h2_transposed(b, b, k - (NT - OWN_H))

            batch(0, True, False)
            with pe.Fori(1, B - 1) as b:
                batch(b, False, False)
            batch(B - 1, False, True)
            values(B - 1, NT - 1)
            for pos in range(4, NT):
                h2_transposed(B - 1, B, pos)
                logits(B - 1 if pos == 4 else B, B, pos - 1)
            logits(B, B, NT - 1)
            ranks(B - 1, B, True)

            pe.wait_ge(table_made, 1)
            pe.wait_ge(expert_in, 16 * 3 * E)

            def experts_of(t, n):
                return nc.values_load_multi_w_load_instructions(
                    tile_exp_i[0:1, bass.ds(t, n)], engines=[mybir.EngineType.PE], min_val=0, max_val=E - 1)[1]

            def rows_t(t, n, arrived, first=False):
                pe.wait_ge(hin_in[n], arrived)
                if not first:
                    pe.wait_ge(hinT_made, t)
                for c in range(DC):
                    mm = pe.transpose(tp[0][:, c * P:(c + 1) * P], hin[:, n, c * P:(c + 1) * P], ident[:, :])
                mm.then_inc(hTp_full, 1)

            def gate_up(t, par, e, early=False):
                pe.wait_ge(hinT_made, t + 1)
                if not early:
                    pe.wait_ge(fused_made, t - 1)
                for w in range(2):
                    for c in range(DC):
                        for x_low, w_low in ((0, 0), (0, 1), (1, 0)):
                            part = low if w_low else high
                            rhs = part[:, bass.ds(e, 1), w, c * F:(c + 1) * F].rearrange("p a f -> p (a f)")
                            mm = pe.matmul(sc[w][:, par * F:(par + 1) * F],
                                           hinT[:, par, x_low, c * P:(c + 1) * P], rhs,
                                           start=(c == 0 and not x_low and not w_low), stop=(c == DC - 1 and x_low == 1))
                mm.then_inc(gu_full, 1)

            def fused_t(t, par, first=False):
                pe.wait_ge(fused_made, t + 1)
                if not first:
                    pe.wait_ge(fusedT_made, t)
                for f in range(FC):
                    mm = pe.transpose(tp[1][:, f * P:(f + 1) * P], fused[:, par, f * P:(f + 1) * P], ident[:, :])
                mm.then_inc(fTp_full, 1)

            def down(t, par, e, early=False):
                pe.wait_ge(fusedT_made, t + 1)
                if not early:
                    pe.wait_ge(y_made, t - 1)
                for f in range(FC):
                    mm = pe.matmul((po if par == 0 else pmisc)[:, 0:D], fusedT[:, par, f * P:(f + 1) * P],
                                   down_sb[:, bass.ds(e, 1), f, :].rearrange("p a d -> p (a d)"),
                                   start=(f == 0), stop=(f == FC - 1))
                mm.then_inc(y_full, 1)

            e = experts_of(0, 3)
            rows_t(0, 0, 16, first=True)
            rows_t(1, 1, 16)
            pe.wait_ge(low_made, 2 * E)
            gate_up(0, 0, e[0], early=True)
            gate_up(1, 1, e[1], early=True)
            fused_t(0, 0, first=True)
            rows_t(2, 2, 16)

            def step(t, u, gate_e, down_e, arrived, early=False):
                gate_up(t + 1, (u + 1) % 2, gate_e)
                fused_t(t, u % 2)
                rows_t(t + 2, (u + 2) % UN, arrived)
                down(t - 1, (u + 1) % 2, down_e, early=early)

            experts = experts_of(0, UN + 2)
            for t in range(1, UN + 1):
                step(t, t % UN, experts[t + 1], experts[t - 1], 16 * ((t + 2) // UN + 1), early=t < 3)
            pe.wait_ge(table_made, 3)
            with pe.Fori(1, LOOPS) as i:
                experts = experts_of(UN * i, UN + 2)
                for u in range(1, UN + 1):
                    step(UN * i + u, u % UN, experts[u + 1], experts[u - 1], 16 * i + 16 * ((u + 2) // UN + 1))
            e = experts_of(TILES - 3, 3)
            gate_up(TILES - 1, (TILES - 1) % 2, e[2])
            fused_t(TILES - 2, (TILES - 2) % 2)
            down(TILES - 3, (TILES - 3) % 2, e[0])
            fused_t(TILES - 1, (TILES - 1) % 2)
            down(TILES - 2, (TILES - 2) % 2, e[1])
            down(TILES - 1, (TILES - 1) % 2, e[2])


_INS = ['L0_attn_x', 'L0_attn_W', 'L0_ffn_router_kernel_DE', 'L0_ffn_kernel_gating_EDF', 'L0_ffn_kernel_up_EDF',
        'L0_ffn_kernel_down_EFD', 'L0_c', 'L0_wmod']
_OUTS = [((B, S, D), 'float32')]


def kernel(**inputs):
    import numpy as _np
    import concourse.bacc as _bacc
    from concourse import mybir as _mybir
    from concourse.bass_utils import run_bass_kernel_spmd as _run

    nc = _bacc.Bacc("TRN2", target_bir_lowering=False, num_devices=1)
    arrays, args = {}, []
    for name in _INS:
        a = _np.ascontiguousarray(inputs[name])
        arrays[f"in_{name}_dram"] = a
        args.append(nc.dram_tensor(f"in_{name}_dram", a.shape, _mybir.dt.from_np(a.dtype), kind="ExternalInput").ap())
    for i, (shape, dtype) in enumerate(_OUTS):
        dt = _mybir.dt.from_np(_np.dtype(dtype))
        args.append(nc.dram_tensor(f"out_{i}_dram", shape, dt, kind="ExternalOutput").ap())
    build(nc, *args)
    r = _run(nc, [arrays], core_ids=[0])
    got = tuple(r.results[0][f"out_{i}_dram"] for i in range(len(_OUTS)))
    return got[0]
```
